# Optimizing a Trainium2 kernel written in Bass

```python
import numpy as np
import jax
import jax.numpy as jnp

def _softmax(x, axis=-1):
    return jax.nn.softmax(x, axis=axis)

def _gelu(x):
    return jax.nn.gelu(x, approximate=True)

def _silu(x):
    return jax.nn.silu(x)

def _sigmoid(x):
    return jax.nn.sigmoid(x)

def _layernorm(x, axis=-1, eps=1e-05):
    m = jnp.mean(x, axis=axis, keepdims=True)
    v = jnp.var(x, axis=axis, keepdims=True)
    return (x - m) / jnp.sqrt(v + eps)

def _scatter_add(tgt, idx, src, axis=0):
    return tgt.at[idx].add(src)

def _segment_sum(src, seg, n):
    return jax.ops.segment_sum(src, seg, n)
kernel_name = 'mk_sandwich_d1_jaxref_r8_51b853'

def setup_inputs(seed: int=0):
    np.random.seed(seed)
    _w = jnp.asarray

    def _L0_attn_setup():
        import jax, jax.numpy as jnp
        import numpy as np
        import math
        D_MODEL = 128
        NUM_HEADS = 16
        D_HEAD = D_MODEL // NUM_HEADS
        BATCH = 4
        SEQ = 256

        def _trunc_normal(key, shape, sd):
            return sd * jax.random.truncated_normal(key, -3.0, 3.0, shape, dtype=jnp.float32)
        key = jax.random.key(seed)
        kx, kq, kk, kv, ko = jax.random.split(key, 5)
        sd = (2.0 / (NUM_HEADS * D_HEAD + D_MODEL)) ** 0.5
        x = jax.random.normal(kx, (BATCH, SEQ, D_MODEL), dtype=jnp.float32)
        WQ = _trunc_normal(kq, (NUM_HEADS, D_HEAD, D_MODEL), sd)
        WK = _trunc_normal(kk, (NUM_HEADS, D_HEAD, D_MODEL), sd)
        WV = _trunc_normal(kv, (NUM_HEADS, D_HEAD, D_MODEL), sd)
        WO = _trunc_normal(ko, (NUM_HEADS, D_MODEL, D_HEAD), sd)
        return {'x': x, 'WQ': WQ, 'WK': WK, 'WV': WV, 'WO': WO}
    _L0_attn_in = _L0_attn_setup()

    def _L0_ffn_setup():
        import jax, jax.numpy as jnp
        import numpy as np
        E, D, F = (8, 128, 512)
        B, S = (4, 256)

        def _layernorm(x, g, b, eps=1e-05):
            mu = jnp.mean(x, axis=-1, keepdims=True)
            var = jnp.var(x, axis=-1, keepdims=True)
            return (x - mu) * jax.lax.rsqrt(var + eps) * g + b
        key = jax.random.key(seed)
        ks = jax.random.split(key, 5)
        return {'input_features': jax.random.normal(ks[0], (B, S, D), jnp.float32), 'centroids': jax.random.normal(ks[1], (E, D), jnp.float32) * 0.1, 'ln_g': jnp.ones((E, D), jnp.float32), 'ln_b': jnp.zeros((E, D), jnp.float32), 'w1': jax.random.normal(ks[2], (E, F, D), jnp.float32) * (1.0 / np.sqrt(D).astype(np.float32)), 'b1': jnp.zeros((E, F), jnp.float32), 'w2': jax.random.normal(ks[3], (E, D, F), jnp.float32) * (1.0 / np.sqrt(F).astype(np.float32)), 'b2': jnp.zeros((E, D), jnp.float32)}
    _L0_ffn_in = _L0_ffn_setup()
    _d = {'L0_attn_x': _L0_attn_in['x'], 'L0_attn_WQ': _L0_attn_in['WQ'], 'L0_attn_WK': _L0_attn_in['WK'], 'L0_attn_WV': _L0_attn_in['WV'], 'L0_attn_WO': _L0_attn_in['WO'], 'L0_ffn_centroids': _L0_ffn_in['centroids'], 'L0_ffn_ln_g': _L0_ffn_in['ln_g'], 'L0_ffn_ln_b': _L0_ffn_in['ln_b'], 'L0_ffn_w1': _L0_ffn_in['w1'], 'L0_ffn_b1': _L0_ffn_in['b1'], 'L0_ffn_w2': _L0_ffn_in['w2'], 'L0_ffn_b2': _L0_ffn_in['b2']}
    _x0 = _d['L0_attn_x']
    _d['L0_attn_x'] = jax.random.normal(jax.random.fold_in(jax.random.key(seed), 1), (16, 256, 128), dtype=_x0.dtype)
    del _x0
    return _d

def reference(L0_attn_x, L0_attn_WQ, L0_attn_WK, L0_attn_WV, L0_attn_WO, L0_ffn_centroids, L0_ffn_ln_g, L0_ffn_ln_b, L0_ffn_w1, L0_ffn_b1, L0_ffn_w2, L0_ffn_b2):

    def _L0_attn_ref(x, WQ, WK, WV, WO):
        import jax, jax.numpy as jnp
        import numpy as np
        import math
        D_MODEL = 128
        NUM_HEADS = 16
        D_HEAD = D_MODEL // NUM_HEADS
        BATCH = 4
        SEQ = 256

        def _trunc_normal(key, shape, sd):
            return sd * jax.random.truncated_normal(key, -3.0, 3.0, shape, dtype=jnp.float32)
        Q = jnp.einsum('bsd,hkd->bhsk', x, WQ)
        K = jnp.einsum('bsd,hkd->bhsk', x, WK)
        V = jnp.einsum('bsd,hkd->bhsk', x, WV)
        d_k = Q.shape[-1]
        scores = jnp.einsum('bhqd,bhkd->bhqk', Q, K) / math.sqrt(d_k)
        seq_len = x.shape[-2]
        causal = jnp.tril(jnp.ones((seq_len, seq_len), dtype=bool))
        scores = jnp.where(causal, scores, -jnp.inf)
        probs = jax.nn.softmax(scores, axis=-1)
        attn = jnp.einsum('bhqk,bhkv->bhqv', probs, V)
        return jnp.einsum('bhsv,hdv->bsd', attn, WO)

    def _L0_ffn_ref(input_features, centroids, ln_g, ln_b, w1, b1, w2, b2):
        import jax, jax.numpy as jnp
        import numpy as np
        E, D, F = (8, 128, 512)
        B, S = (4, 256)

        def _layernorm(x, g, b, eps=1e-05):
            mu = jnp.mean(x, axis=-1, keepdims=True)
            var = jnp.var(x, axis=-1, keepdims=True)
            return (x - mu) * jax.lax.rsqrt(var + eps) * g + b
        Bf, Sf, Df = input_features.shape
        x = input_features.reshape(-1, Df)
        aff = x @ centroids.T
        assign = jnp.argmax(aff, axis=1)
        order = jnp.argsort(assign)
        xs = x[order]
        es = assign[order]
        alpha = jax.nn.sigmoid(jnp.take_along_axis(aff[order], es[:, None], axis=1))
        nE = centroids.shape[0]
        y = jnp.zeros_like(xs)
        for e in range(nE):
            h = _layernorm(xs, ln_g[e], ln_b[e])
            h = jax.nn.relu(h @ w1[e].T + b1[e])
            ye = xs + h @ w2[e].T + b2[e]
            y = y + jnp.where((es == e)[:, None], ye, 0.0)
        out_sorted = alpha * y + (1.0 - alpha) * xs
        inv = jnp.argsort(order)
        return out_sorted[inv].reshape(Bf, Sf, Df)
    x = L0_attn_x
    x = x + _layernorm(_L0_attn_ref(_layernorm(x, axis=-1), L0_attn_WQ, L0_attn_WK, L0_attn_WV, L0_attn_WO), axis=-1)
    x = x + _layernorm(_L0_ffn_ref(_layernorm(x, axis=-1), L0_ffn_centroids, L0_ffn_ln_g, L0_ffn_ln_b, L0_ffn_w1, L0_ffn_b1, L0_ffn_w2, L0_ffn_b2), axis=-1)
    return x

_drawn_inputs = setup_inputs


def setup_inputs(seed=0):
    import zlib

    import numpy as np

    out = dict(_drawn_inputs(seed))
    spreads = {'L0_ffn_ln_g': (1.0, 0.2),
     'L0_ffn_ln_b': (0.0, 0.368),
     'L0_ffn_b1': (0.0, 0.375),
     'L0_ffn_b2': (0.0, 0.271)}
    factors = {}
    for name, (base, spread) in spreads.items():
        noise = np.random.default_rng([zlib.crc32(name.encode()), seed]).standard_normal(out[name].shape)
        drawn = base * np.exp(spread * noise) if base else spread * noise
        out[name] = jnp.asarray(drawn.astype(out[name].dtype))
    for name, factor in factors.items():
        out[name] = (out[name] * factor).astype(out[name].dtype)
    return out
```

```python
from contextlib import ExitStack

import numpy as np

import concourse.bass as bass
from concourse import mybir

ALU = mybir.AluOpType
ACT = mybir.ActivationFunctionType
AX_X = mybir.AxisListType.X
F32 = mybir.dt.float32
BF16 = mybir.dt.bfloat16
I32 = mybir.dt.int32
U32 = mybir.dt.uint32

P = 128
EPS = 1e-5
NEG = -1e30


class Batch:

    def __init__(self, k, trip=None):
        self.k, self.trip = k, trip

    def plus(self, n):
        return Batch(self.k + n, self.trip)

    def times(self, a, b=0):
        return a * self.k + b if self.trip is None else self.trip * (2 * a) + (a * self.k + b)

    def turns(self, a, b=0):
        return a * (self.k // 2) + b if self.trip is None else self.trip * a + (a * (self.k // 2) + b)

    def follows(self, n):
        return self.k >= n

    @property
    def parity(self):
        return self.k % 2


def sandwich_kernel(nc, x, attn_w, w1t, w2t, ln_cols, b1_cols, b2, cent_t, out):
    B, SEQ, D = x.shape
    NH = 16
    DH = D // NH
    E, _, F = w1t.shape
    NT = B * SEQ // P
    FC = F // P
    NG = NH // 4
    SCALE = float(DH) ** -0.5
    ST = NT + E
    ROW = D + 1
    SP1 = F + 2 + FC
    assert D == P and SEQ == 2 * P and B % 2 == 0

    xs_dram = nc.dram_tensor("xs_rows", (ST * P, ROW), F32, kind="Internal").ap()
    z_dram = nc.dram_tensor("z_rows", (NT * P + ST * P, D), F32, kind="Internal").ap()
    qk_dram = nc.dram_tensor("qk_parts", (2, 3, 2, NH, DH, SEQ), BF16, kind="Internal").ap()
    sh_dram = nc.dram_tensor("shift_rows", (2, 2, 2, 8 * SEQ), BF16, kind="Internal").ap()

    with ExitStack() as ctx:
        def sb(name, shape, dt=F32):
            return ctx.enter_context(nc.sbuf_tensor(name, shape, dt))

        def ps(name, shape, dt=F32):
            return ctx.enter_context(nc.psum_tensor(name, shape, dt))

        def sem(name):
            return ctx.enter_context(nc.semaphore(name))

        wat = sb("wat", [P, 4, D])
        w1_tab = sb("w1_tab", [P, E, SP1])
        w2_tab = sb("w2_tab", [P, E * FC * D])
        b2_tab = sb("b2_tab", [P, E * D])
        cent = sb("cent", [P, E])
        ident = sb("ident", [P, P])
        identb = sb("identb", [P, P], BF16)
        causal = sb("causal", [P, 4, P], BF16)
        before = sb("before", [P, P], BF16)
        onesb = sb("onesb", [P, P], BF16)
        mhalf = sb("mhalf", [P, NT])
        x_all = sb("x_all", [P, NT, D])
        y_all = sb("y_all", [P, NT, D])
        late = sb("late", [P, NT * (D + ROW)])
        f_all = late[:, 0:NT * D].rearrange("p (t d) -> p t d", d=D)
        pay = late[:, NT * D:].rearrange("p (t d) -> p t d", d=ROW)
        fill = late[:, 0:ST * ROW].rearrange("p (t d) -> p t d", d=ROW)
        stat = sb("stat", [P, NT, 6])
        mv = sb("mv", [P, NT, 2])
        ve = sb("ve", [P, NT])
        rstd = sb("rstd", [P, NT])
        xn = sb("xn", [P, 2, 2, D])
        xnT = sb("xnT", [P, 2, SEQ])
        qkp = sb("qkp", [P, 2, 3, 2, SEQ], BF16)
        res1 = sb("res1", [P, 2 * SEQ])
        qaug = sb("qaug", [P, 2, NH, SEQ], BF16)
        kaug = sb("kaug", [P, 2, NH, SEQ], BF16)
        nmf = sb("nmf", [P, 2, NH, 2])
        nmp = sb("nmp", [P, 2, 2, 2, 16], BF16)
        nmT = sb("nmT", [32, 2, 2, P], BF16)
        vaug = sb("vaug", [P, 2, 2, NH, 32])
        p0 = sb("p0", [P, 2, 4, SEQ])
        p1 = sb("p1", [P, 2, 4, P])
        oT = sb("oT", [P, 4, SEQ])
        rden = sb("rden", [P, 2, NH])
        on = sb("on", [P, 2, NH, DH])
        onT = sb("onT", [P, SEQ])
        fT = sb("fT", [P, 2, 4, P])
        aff = sb("aff", [P, NT, E])
        amax = sb("amax", [P, NT])
        alpha = sb("alpha", [P, NT])
        eneg = sb("eneg", [P, NT])
        hot = sb("hot", [P, NT, E])
        hotb = sb("hotb", [P, NT, E], BF16)
        key = sb("key", [P, NT])
        down = sb("down", [P, E])
        cnt = sb("cnt", [P, 2, NT, E])
        base = sb("base", [P, NT, E])
        total = sb("total", [P, E])
        steps = sb("steps", [P, NT])
        slots = sb("slots", [P, ST])
        above = sb("above", [P, E, NT])
        ntile = sb("ntile", [P, 4, E])
        tstart = sb("tstart", [P, E])
        over = sb("over", [P, ST, E])
        esel = sb("esel", [P, ST])
        eidx = sb("eidx", [P, ST], I32)
        posf = sb("posf", [P, NT])
        pos = sb("pos", [P, NT], I32)
        tokid = sb("tokid", [P, NT], I32)
        dumpid = sb("dumpid", [P, ST], I32)
        xs = sb("xs", [P, 2, ROW])
        w1s = sb("w1s", [P, 2, SP1])
        nT = sb("nT", [P, 2, P])
        hs = sb("hs", [P, 2, FC, P])
        zo = sb("zo", [P, 2, D])

        S = ps("S", [P, 2, 512])
        ST0 = ps("ST0", [P, 4, SEQ])
        ST1 = ps("ST1", [P, 4, P])
        O = ps("O", [P, 2, 2, SEQ])
        M = ps("M", [P, 512])

        names = ("w_attn w_ffn x_in aug0 zero_w ids consts pmem dmem vmem kmem "
                 "st_x agg_x ve_x rs_x xn_r xnT_r xnT_d qk_r hi_d r1_d mid_d parts_d "
                 "v_r v_d s_r red nm_hi nm_d shT_r sh_d st0_r st1_r exp0 exp1 sel0 sel1 pv o_ev "
                 "otr_r rden_d on_d onT_r onT_d y_r y_d "
                 "lnc rs_b fT_r fT_d aff_r ex_d hot_d cnt_r rt pos_d scat "
                 "w1_d xsT_r nT_d h_r ha_d hd_d z_r zo_d "
                 "z_in out_w tl").split()
        s = {n: sem(n) for n in names}
        qk_w = [sem(f"qk_w{p}") for p in (0, 1)]
        aug_in = [sem(f"aug_in{p}") for p in (0, 1)]
        sh_w = [sem(f"sh_w{h}") for h in (0, 1)]
        sh_in = [sem(f"sh_in{h}") for h in (0, 1)]
        xs_in = [sem(f"xs_in{p}") for p in (0, 1)]
        z_sc = [sem(f"z_sc{p}") for p in (0, 1)]
        out_s = [sem(f"out_s{p}") for p in (0, 1)]

        block = ctx.enter_context(nc.Block())
        LAST = B - 1

        def hidden(p, c):
            return S[:, p, c * P:(c + 1) * P] if c < FC // 2 else ST0[:, 2 * p:2 * p + 2].rearrange("p a n -> p (a n)")[
                :, (c - FC // 2) * P:(c - FC // 2 + 1) * P]

        Q_SRC, K_SRC = (0, 0, 0, 1, 1, 2), (0, 1, 2, 0, 1, 0)
        NPROD = len(Q_SRC) * DH
        NS = P - 2

        def wait_batch(eng, name, value):
            if not isinstance(value, int):
                value = eng.compute_val(value)
            eng.wait_ge(s["consts"], 1)
            eng.wait_ge(name, value)

        def iterations(eng, step):
            for i in range(3):
                step(Batch(i))
            with eng.Fori(0, (B - 6) // 2) as trip:
                step(Batch(3, trip))
                step(Batch(4, trip))
            for i in range(B - 3, B + 1):
                step(Batch(i))

        @block.sync
        def _(sp):
            xv = x.rearrange("b (t p) d -> p (b t) d", p=P)
            sp.dma_start(x_all[:, :, :], xv).then_inc(s["x_in"], 16)
            sp.dma_start(wat[:, :, :], attn_w.rearrange("k p n -> p k n")).then_inc(s["w_attn"], 16)

            def parts_out(b):
                p = b.parity
                wait_batch(sp, s["parts_d"], b.times(1, 1))
                if b.follows(2):
                    wait_batch(sp, aug_in[p], b.turns(192))
                sp.dma_start(qk_dram[p].rearrange("c s h d t -> (h d) c s t"), qkp[:, p]).then_inc(qk_w[p], 16)

            def parts_in(b):
                p = b.parity
                wait_batch(sp, qk_w[p], b.turns(16, 16))
                if b.follows(2):
                    wait_batch(sp, s["st1_r"], b.times(4, -4))
                for side, (dst, src) in enumerate(((qaug, Q_SRC), (kaug, K_SRC))):
                    for r, c in enumerate(src):
                        sp.dma_start(dst[r * DH:(r + 1) * DH, p],
                                     qk_dram[p, c, side].rearrange("h d t -> d h t")).then_inc(aug_in[p], 16)

            def shift(b, half):
                wait_batch(sp, s["sh_d"], b.times(2, half + 1))
                if b.follows(2):
                    wait_batch(sp, sh_in[half], b.times(16, -16))
                sp.dma_start(sh_dram[b.parity, half].rearrange("c (r t) -> (c r) t", t=P),
                             nmT[:, b.parity, half]).then_inc(sh_w[half], 16)
                wait_batch(sp, sh_w[half], b.times(16, 16))
                if b.follows(2):
                    wait_batch(sp, s["st1_r"], b.times(4, -4))
                sp.dma_start(qaug[NS:P, b.parity, 8 * half:8 * half + 8],
                             sh_dram[b.parity, half].rearrange("c (h t) -> c h t", t=SEQ)).then_inc(sh_in[half], 16)

            parts_out(Batch(0))
            sp.wait_ge(s["aug0"], 4)
            parts_in(Batch(0))
            parts_out(Batch(1))
            parts_in(Batch(1))
            for e in range(E):
                sp.dma_start(w1_tab[:, e, 0:F], w1t[e]).then_inc(s["w_ffn"], 16)
            sp.dma_start(w1_tab[:, :, F:F + 2], ln_cols).then_inc(s["w_ffn"], 16)
            sp.dma_start(w1_tab[:, :, F + 2:SP1], b1_cols).then_inc(s["w_ffn"], 16)
            sp.dma_start(w2_tab[:, :], w2t).then_inc(s["w_ffn"], 16)
            sp.dma_start(b2_tab[:, :], b2.rearrange("(o e) d -> o (e d)", o=1).to_broadcast([P, E * D])).then_inc(s["w_ffn"], 16)
            sp.dma_start(cent[:, :], cent_t).then_inc(s["w_ffn"], 16)
            sp.wait_ge(s["ids"], 3)
            sp.dma_start(xs_dram.rearrange("(t p) d -> p t d", p=P), fill[:, :, :]).then_inc(s["zero_w"], 16)
            shift(Batch(0), 0)

            def step(i):
                if i.k <= LAST:
                    shift(i, 1)
                if i.k + 2 <= LAST:
                    parts_out(i.plus(2))
                if i.k + 1 <= LAST:
                    shift(i.plus(1), 0)
                if i.k + 2 <= LAST:
                    parts_in(i.plus(2))

            iterations(sp, step)

            sp.wait_ge(s["scat"], 16 * NT)

            def rows_in(t, p, first):
                if not first:
                    wait_batch(sp, z_sc[p], t * 16)
                    wait_batch(sp, s["xsT_r"], t * 2 + (p - 1))
                sp.dma_start(xs[:, p], xs_dram[bass.ds(t * (2 * P) + p * P, P), :]).then_inc(xs_in[p], 16)

            rows_in(0, 0, True)
            rows_in(0, 1, True)
            with sp.Fori(1, ST // 2) as t:
                rows_in(t, 0, False)
                rows_in(t, 1, False)
            sp.wait_ge(z_sc[0], 8 * ST)
            sp.wait_ge(z_sc[1], 8 * ST)
            sp.dma_start(y_all[:, :, :], z_dram[0:NT * P, :].rearrange("(t p) d -> p t d", p=P)).then_inc(s["z_in"], 16)
            ov = out.rearrange("b (t p) d -> p (b t) d", p=P)
            with sp.Fori(0, NT // 4) as c:
                wait_batch(sp, s["out_w"], c + 1)
                sp.dma_start(ov[:, bass.ds(c * 4, 4), :], x_all[:, bass.ds(c * 4, 4), :]).then_inc(out_s[0], 16)
            sp.wait_ge(out_s[0], 16 * (NT // 4))

        @block.gpsimd
        def _(pool):
            g = nc.gpsimd
            g.memset(ident[:, :], 0.0).then_inc(s["pmem"], 1)
            g.memset(causal[:, :, :], 0.0).then_inc(s["pmem"], 1)
            g.memset(before[:, :], 1.0).then_inc(s["pmem"], 1)
            g.memset(onesb[:, :], 1.0).then_inc(s["consts"], 1)
            g.memset(mhalf[:, :], -0.5).then_inc(s["consts"], 1)
            pool.wait_ge(s["pmem"], 3)
            g.affine_select(out=ident[:, :], in_=ident[:, :], compare_op=ALU.not_equal, fill=1.0, base=0,
                            pattern=[[-1, P]], channel_multiplier=1).then_inc(s["pmem"], 1)
            g.affine_select(out=causal[:, :, :], in_=causal[:, :, :], compare_op=ALU.is_ge, fill=NEG, base=0,
                            pattern=[[0, 4], [-1, P]], channel_multiplier=1).then_inc(s["consts"], 1)
            g.affine_select(out=before[:, :], in_=before[:, :], compare_op=ALU.is_gt, fill=0.0, base=0,
                            pattern=[[1, P]], channel_multiplier=-1).then_inc(s["consts"], 1)
            pool.wait_ge(s["pmem"], 4)
            g.tensor_copy(identb[:, :], ident[:, :]).then_inc(s["consts"], 1)
            pool.wait_ge(s["ve_x"], 1)
            g.tensor_tensor(rstd[:, :], ve[:, :], mhalf[:, :], op=ALU.pow).then_inc(s["rs_x"], 1)
            g.memset(kaug[:, 0], 0.0).then_inc(s["kmem"], 1)
            g.memset(kaug[:, 1], 0.0).then_inc(s["kmem"], 1)
            pool.wait_ge(s["kmem"], 2)
            for p in (0, 1):
                g.affine_select(out=kaug[:, p], in_=kaug[:, p], compare_op=ALU.is_ge, fill=1.0, base=NS - 1,
                                pattern=[[0, NH], [0, SEQ]], channel_multiplier=-1).then_inc(s["aug0"], 1)

            def parts(b):
                p = b.parity
                if b.follows(2):
                    wait_batch(pool, qk_w[p], b.turns(16))
                wait_batch(pool, s["r1_d"], b.times(1, 1))
                g.tensor_copy(qkp[:, p, 1].rearrange("p s t -> p (s t)"), res1[:, :]).then_inc(s["mid_d"], 1)
                wait_batch(pool, s["mid_d"], b.times(1, 1))
                g.tensor_tensor(qkp[:, p, 2].rearrange("p s t -> p (s t)"), res1[:, :],
                                qkp[:, p, 1].rearrange("p s t -> p (s t)"), op=ALU.subtract).then_inc(s["parts_d"], 1)

            def select(i, gr):
                v = p0[:, gr % 2, :, 0:P]
                wait_batch(pool, s["exp0"], i.times(NG, gr + 1))
                g.affine_select(out=v, in_=v, compare_op=ALU.is_ge, fill=0.0, base=0,
                                pattern=[[0, 4], [1, P]], channel_multiplier=-1).then_inc(s["sel0"], 1)
                wait_batch(pool, s["exp1"], i.times(NG, gr + 1))
                v = p1[:, gr % 2]
                g.affine_select(out=v, in_=v, compare_op=ALU.is_ge, fill=0.0, base=0,
                                pattern=[[0, 4], [1, P]], channel_multiplier=-1).then_inc(s["sel1"], 1)

            parts(Batch(0))
            parts(Batch(1))
            g.iota(tokid[:, :], [[P, NT]], base=0, channel_multiplier=1).then_inc(s["ids"], 1)
            g.iota(dumpid[:, :], [[P, ST]], base=NT * P, channel_multiplier=1).then_inc(s["dmem"], 1)
            g.iota(down[:, :], [[-1, E]], base=E, channel_multiplier=0,
                   allow_small_or_imprecise_dtypes=True).then_inc(s["consts"], 1)
            g.iota(steps[:, :], [[P, NT]], base=0, channel_multiplier=0,
                   allow_small_or_imprecise_dtypes=True).then_inc(s["consts"], 1)
            g.iota(slots[:, :], [[1, ST]], base=0, channel_multiplier=0,
                   allow_small_or_imprecise_dtypes=True).then_inc(s["consts"], 1)
            g.memset(fill[:, :, 0:D], 0.0).then_inc(s["ids"], 1)
            pool.wait_ge(s["dmem"], 1)
            g.tensor_copy(fill[:, :, D:ROW].bitcast(I32).rearrange("p t o -> p (t o)"), dumpid[:, :]).then_inc(s["ids"], 1)

            def step(i):
                if i.k <= LAST:
                    select(i, 0)
                    select(i, 1)
                if i.k + 2 <= LAST:
                    parts(i.plus(2))
                if i.k <= LAST:
                    select(i, 2)
                    select(i, 3)

            iterations(pool, step)

            for n in range(3):
                pool.wait_ge(s["lnc"], n + 1)
                g.tensor_tensor(rstd[:, :], ve[:, :], mhalf[:, :], op=ALU.pow).then_inc(s["rs_b"], 1)
            pool.wait_ge(s["pos_d"], 1)
            pool.wait_ge(s["zero_w"], 16)
            for t in range(NT):
                g.indirect_dma_start(out=xs_dram, out_offset=bass.IndirectOffsetOnAxis(ap=pos[:, t:t + 1].bitcast(U32), axis=0),
                                     in_=pay[:, t, :], in_offset=None).then_inc(s["scat"], 16)

            def rows_out(t, p):
                wait_batch(pool, s["zo_d"], t * 2 + (p + 1))
                g.indirect_dma_start(out=z_dram, out_offset=bass.IndirectOffsetOnAxis(ap=xs[:, p, D:ROW].bitcast(U32), axis=0),
                                     in_=zo[:, p, :], in_offset=None).then_inc(z_sc[p], 16)

            with pool.Fori(0, ST // 2) as t:
                rows_out(t, 0)
                rows_out(t, 1)
            pool.wait_ge(s["lnc"], 4)
            g.tensor_tensor(rstd[:, :], ve[:, :], mhalf[:, :], op=ALU.pow).then_inc(s["rs_b"], 1)

        @block.scalar
        def _(act):
            a = nc.scalar

            def xnT_out(b):
                p = b.parity
                act.wait_ge(s["xnT_r"], b.times(1, 1))
                if b.follows(2):
                    act.wait_ge(s["v_r"], b.times(1, -1))
                a.activation(xnT[:, p], M[:, 0:SEQ], ACT.Copy).then_inc(s["xnT_d"], 1)

            def high(b):
                p = b.parity
                act.wait_ge(s["qk_r"], b.times(1, 1))
                if b.follows(2):
                    act.wait_ge(qk_w[p], b.turns(16))
                a.activation(qkp[:, p, 0].rearrange("p s t -> p (s t)"), M[:, :], ACT.Copy).then_inc(s["hi_d"], 1)

            def shift_out(b, half):
                act.wait_ge(s["shT_r"], b.times(2, half + 1))
                if b.follows(2):
                    act.wait_ge(sh_w[half], b.times(16, -16))
                a.activation(nmT[:, b.parity, half], M[:, 0:P // 2].bitcast(BF16)[0:32, 0:P], ACT.Copy).then_inc(s["sh_d"], 1)

            def exps(i, gr):
                act.wait_ge(s["st0_r"], i.times(NG, gr + 1))
                if i.k > 0 or gr >= 2:
                    act.wait_ge(s["pv"], i.times(NG, gr - 1))
                a.activation(p0[:, gr % 2], ST0[:, :, :], ACT.Exp, scale=SCALE).then_inc(s["exp0"], 1)
                act.wait_ge(s["st1_r"], i.times(NG, gr + 1))
                a.activation(p1[:, gr % 2], ST1[:, :, :], ACT.Exp, scale=SCALE).then_inc(s["exp1"], 1)

            def o_out(i, half):
                act.wait_ge(s["pv"], i.times(NG, 2 * half + 2))
                if i.follows(1):
                    act.wait_ge(s["otr_r"], i.times(2))
                a.activation(oT[:, 2 * half:2 * half + 2], O[:, half], ACT.Copy).then_inc(s["o_ev"], 1)

            xnT_out(Batch(0))
            high(Batch(0))
            xnT_out(Batch(1))
            high(Batch(1))
            shift_out(Batch(0), 0)

            def step(i):
                if i.k <= LAST:
                    exps(i, 0)
                if i.k >= 1:
                    o_out(i.plus(-1), 1)
                if i.k <= LAST:
                    shift_out(i, 1)
                if i.k + 2 <= LAST:
                    xnT_out(i.plus(2))
                if i.k <= LAST:
                    exps(i, 1)
                if i.k + 2 <= LAST:
                    high(i.plus(2))
                if i.k <= LAST:
                    exps(i, 2)
                if i.k + 1 <= LAST:
                    shift_out(i.plus(1), 0)
                if i.k <= LAST:
                    o_out(i, 0)
                    exps(i, 3)
                if i.k >= 1:
                    act.wait_ge(s["onT_r"], i.times(1))
                    a.activation(onT[:, :], M[:, 0:SEQ], ACT.Copy).then_inc(s["onT_d"], 1)

            iterations(act, step)

            for c in range(NT // 4):
                act.wait_ge(s["fT_r"], c + 1)
                if c >= 2:
                    act.wait_ge(s["aff_r"], c - 1)
                a.activation(fT[:, c % 2], S[:, c % 2].rearrange("p (t n) -> p t n", n=P), ACT.Copy).then_inc(s["fT_d"], 1)
            act.wait_ge(s["hot_d"], 1)
            a.activation(eneg[:, :], amax[:, :], ACT.Exp, scale=-1.0).then_inc(s["ex_d"], 1)

            def tile(t, p, first):
                act.wait_ge(s["w1_d"], t * 2 + (p + 1))
                act.wait_ge(s["xsT_r"], t * 2 + (p + 1))
                a.activation(nT[:, p], M[:, 0:P], ACT.Identity, scale=w1s[:, p, F:F + 1],
                             bias=w1s[:, p, F + 1:F + 2]).then_inc(s["nT_d"], 1)
                act.wait_ge(s["h_r"], t * 4 + (2 * p + 1))
                if not first:
                    act.wait_ge(s["z_r"], t * 2 + (p - 1))
                for c in range(FC // 2):
                    last = a.activation(hs[:, p, c], hidden(p, c), ACT.Relu,
                                        bias=w1s[:, p, F + 2 + c:F + 3 + c])
                last.then_inc(s["ha_d"], 1)

            tile(0, 0, True)
            tile(0, 1, True)
            with act.Fori(1, ST // 2) as t:
                tile(t, 0, False)
                tile(t, 1, False)

        @block.tensor
        def _(pe):
            mm = nc.tensor.matmul
            m_free = [None]

            def take_m():
                if m_free[0]:
                    for name, value in m_free[0]:
                        pe.wait_ge(s[name], value)

            def transpose_x(b):
                take_m()
                pe.wait_ge(s["xn_r"], b.times(1, 1))
                for t in (0, 1):
                    last = nc.tensor.transpose(M[:, t * P:(t + 1) * P], xn[:, b.parity, t], ident[:, :])
                last.then_inc(s["xnT_r"], 1)
                m_free[0] = [("xnT_d", b.times(1, 1))]

            def project_qk(b):
                take_m()
                pe.wait_ge(s["xnT_d"], b.times(1, 1))
                for w in (0, 1):
                    last = mm(M[:, w * SEQ:(w + 1) * SEQ], wat[:, w], xnT[:, b.parity], start=True, stop=True)
                last.then_inc(s["qk_r"], 1)
                m_free[0] = [("hi_d", b.times(1, 1)), ("r1_d", b.times(1, 1))]

            def project_v(b):
                take_m()
                for t in (0, 1):
                    last = mm(M[:, t * P:(t + 1) * P], xnT[:, b.parity, t * P:(t + 1) * P], wat[:, 2],
                              start=True, stop=True)
                last.then_inc(s["v_r"], 1)
                m_free[0] = [("v_d", b.times(1, 1))]

            def transpose_shift(b, half):
                take_m()
                pe.wait_ge(s["nm_d"], b.times(2, half + 1))
                nc.tensor.transpose(M[:, 0:P // 2].bitcast(BF16)[0:32, 0:P],
                                    nmp[:, b.parity, half].rearrange("p c r -> p (c r)"), identb[:, :]).then_inc(s["shT_r"], 1)
                m_free[0] = [("sh_d", b.times(2, half + 1))]

            def scores_by_query(b, gr):
                p = b.parity
                if gr == 0:
                    pe.wait_ge(aug_in[p], b.turns(192, 192))
                for u in range(3):
                    n = 3 * gr + u
                    if b.k > 0 or n >= 2:
                        pe.wait_ge(s["red"], b.times(12, n - 1))
                    bank = S[:, n % 2]
                    if u == 0:
                        mm(bank, identb[:, :], causal[:, :, :], start=True, stop=False)
                        for j in range(4):
                            h = 4 * gr + j
                            last = mm(bank[:, j * P:(j + 1) * P], qaug[0:NS, p, h, 0:P], kaug[0:NS, p, h, 0:P],
                                      start=False, stop=(j == 3))
                    else:
                        mm(bank.rearrange("p (j c n) -> p j c n", j=2, c=2)[:, :, 1], identb[:, :], causal[:, 0:2],
                           start=True, stop=False)
                        for j in range(2):
                            h = 4 * gr + 2 * (u - 1) + j
                            for kb in (0, 1):
                                last = mm(bank[:, j * SEQ + kb * P:j * SEQ + (kb + 1) * P], qaug[0:NS, p, h, P:SEQ],
                                          kaug[0:NS, p, h, kb * P:(kb + 1) * P], start=False, stop=(j == 1 and kb == 1))
                    last.then_inc(s["s_r"], 1)

            def scores_by_key(i, gr):
                p = i.parity
                if gr % 2 == 0:
                    pe.wait_ge(sh_in[gr // 2], i.times(16, 16))
                if i.k > 0 or gr > 0:
                    pe.wait_ge(s["exp0"], i.times(NG, gr))
                for j in range(4):
                    h = 4 * gr + j
                    last = mm(ST0[:, j], kaug[:, p, h, 0:P], qaug[:, p, h], start=True, stop=True)
                last.then_inc(s["st0_r"], 1)
                if i.k > 0 or gr > 0:
                    pe.wait_ge(s["exp1"], i.times(NG, gr))
                for j in range(4):
                    h = 4 * gr + j
                    last = mm(ST1[:, j], kaug[:, p, h, P:SEQ], qaug[:, p, h, P:SEQ], start=True, stop=True)
                last.then_inc(s["st1_r"], 1)

            def weigh_values(i, gr):
                p = i.parity
                if gr == 0:
                    pe.wait_ge(s["v_d"], i.times(1, 1))
                if i.k > 0 and gr % 2 == 0:
                    pe.wait_ge(s["o_ev"], i.times(2, gr // 2 - 1))
                pe.wait_ge(s["sel0"], i.times(NG, gr + 1))
                for j in range(4):
                    mm(O[32 * j:32 * j + 32, gr // 2, gr % 2, :], vaug[:, p, 0, 4 * gr + j], p0[:, gr % 2, j],
                       start=True, stop=False)
                pe.wait_ge(s["sel1"], i.times(NG, gr + 1))
                for j in range(4):
                    last = mm(O[32 * j:32 * j + 32, gr // 2, gr % 2, P:SEQ], vaug[:, p, 1, 4 * gr + j], p1[:, gr % 2, j],
                              start=False, stop=True)
                last.then_inc(s["pv"], 1)

            def transpose_o(i, qb):
                take_m()
                pe.wait_ge(s["o_ev"], i.times(2, 2))
                for gr in range(NG):
                    last = nc.tensor.transpose(M[:, gr * P:(gr + 1) * P], oT[:, gr, qb * P:(qb + 1) * P], ident[:, :])
                last.then_inc(s["otr_r"], 1)
                m_free[0] = [("on_d", i.times(2, qb + 1))]

            def transpose_on(i):
                take_m()
                for qb in (0, 1):
                    last = nc.tensor.transpose(M[:, qb * P:(qb + 1) * P], on[:, qb].rearrange("p h v -> p (h v)"), ident[:, :])
                last.then_inc(s["onT_r"], 1)
                m_free[0] = [("onT_d", i.times(1, 1))]

            def project_o(i):
                take_m()
                for qb in (0, 1):
                    last = mm(M[:, qb * P:(qb + 1) * P], onT[:, qb * P:(qb + 1) * P], wat[:, 3], start=True, stop=True)
                last.then_inc(s["y_r"], 1)
                m_free[0] = [("y_d", i.times(1, 1))]

            pe.wait_ge(s["consts"], 5)
            pe.wait_ge(s["w_attn"], 16)
            transpose_x(Batch(0))
            project_qk(Batch(0))
            project_v(Batch(0))
            transpose_x(Batch(1))
            project_qk(Batch(1))
            pe.wait_ge(s["aug0"], 4)
            for gr in range(NG):
                scores_by_query(Batch(0), gr)
                if gr == 1:
                    transpose_shift(Batch(0), 0)

            def step(i):
                if i.k >= 1:
                    m_free[0] = [("y_d", i.times(1, -1))] if i.k > 1 else [("v_d", 2)]
                if i.k <= LAST:
                    scores_by_key(i, 0)
                if i.k >= 1:
                    weigh_values(i.plus(-1), 3)
                if i.k <= LAST:
                    transpose_shift(i, 1)
                if i.k + 1 <= LAST:
                    scores_by_query(i.plus(1), 0)
                if i.k + 2 <= LAST:
                    transpose_x(i.plus(2))
                if i.k <= LAST:
                    scores_by_key(i, 1)
                if i.k >= 1:
                    transpose_o(i.plus(-1), 0)
                if i.k + 1 <= LAST:
                    scores_by_query(i.plus(1), 1)
                if i.k <= LAST:
                    weigh_values(i, 0)
                if i.k + 2 <= LAST:
                    project_qk(i.plus(2))
                if i.k <= LAST:
                    scores_by_key(i, 2)
                if i.k >= 1:
                    transpose_o(i.plus(-1), 1)
                if i.k + 1 <= LAST:
                    transpose_shift(i.plus(1), 0)
                    scores_by_query(i.plus(1), 2)
                if i.k <= LAST:
                    weigh_values(i, 1)
                if i.k + 1 <= LAST:
                    project_v(i.plus(1))
                if i.k <= LAST:
                    scores_by_key(i, 3)
                if i.k >= 1:
                    transpose_on(i.plus(-1))
                if i.k + 1 <= LAST:
                    scores_by_query(i.plus(1), 3)
                if i.k <= LAST:
                    weigh_values(i, 2)
                if i.k >= 1:
                    project_o(i.plus(-1))

            iterations(pe, step)

            pe.wait_ge(s["w_ffn"], 16 * (E + 5))
            pe.wait_ge(s["lnc"], 3)
            for c in range(NT // 4):
                if c >= 2:
                    pe.wait_ge(s["fT_d"], c - 1)
                for t in range(4):
                    last = nc.tensor.transpose(S[:, c % 2, t * P:(t + 1) * P], f_all[:, 4 * c + t], ident[:, :])
                last.then_inc(s["fT_r"], 1)
                pe.wait_ge(s["fT_d"], c + 1)
                for t in range(4):
                    n = 4 * c + t
                    last = mm(M[:, n * E:(n + 1) * E], fT[:, c % 2, t], cent[:, :], start=True, stop=True)
                last.then_inc(s["aff_r"], 1)
            pe.wait_ge(s["hot_d"], 1)
            hb = hotb[:, :, :].rearrange("p t e -> p (t e)")
            mm(M[:, 0:NT * E], before[:, :], hb, start=True, stop=True)
            mm(M[:, NT * E:2 * NT * E], onesb[:, :], hb, start=True, stop=True).then_inc(s["cnt_r"], 1)
            pe.wait_ge(s["rt"], 1)

            def up(t, p, first):
                e = expert_of(t, p)
                pe.wait_ge(xs_in[p], t * 16 + 16)
                if p == 1 or not first:
                    pe.wait_ge(s["nT_d"], t * 2 + p)
                nc.tensor.transpose(M[:, 0:P], xs[:, p, 0:D], ident[:, :]).then_inc(s["xsT_r"], 1)
                pe.wait_ge(s["nT_d"], t * 2 + (p + 1))
                if not first:
                    pe.wait_ge(s["ha_d"], t * 2 + (p - 1))
                    pe.wait_ge(s["hd_d"], t * 2 + (p - 1))
                for c in range(FC):
                    last = mm(hidden(p, c), w1s[:, p, c * P:(c + 1) * P], nT[:, p], start=True, stop=True)
                    if c % 2:
                        last.then_inc(s["h_r"], 1)
                return e

            def expert_of(t, p):
                return pe.value_load(eidx[0:1, bass.ds(t * 2 + p, 1)], min_val=0, max_val=E - 1)

            def down_(t, p, e, first):
                pe.wait_ge(s["ha_d"], t * 2 + (p + 1))
                if not first:
                    pe.wait_ge(s["zo_d"], t * 2 + (p - 1))
                for c in range(FC):
                    if c == FC // 2:
                        pe.wait_ge(s["hd_d"], t * 2 + (p + 1))
                    last = mm(O[:, p, 0, 0:D], hs[:, p, c], w2_tab[:, bass.ds(e * (FC * D) + c * D, D)],
                              start=(c == 0), stop=(c == FC - 1))
                last.then_inc(s["z_r"], 1)

            e0 = up(0, 0, True)
            e1 = up(0, 1, True)
            down_(0, 0, e0, True)
            down_(0, 1, e1, True)
            with pe.Fori(1, ST // 2) as t:
                e0 = up(t, 0, False)
                e1 = up(t, 1, False)
                down_(t, 0, e0, False)
                down_(t, 1, e1, False)

        @block.vector
        def _(dve):
            v = nc.vector
            dve.wait_ge(s["x_in"], 16)
            v.memset(qaug[:, 0], 0.0).then_inc(s["aug0"], 1)
            v.memset(qaug[:, 1], 0.0).then_inc(s["aug0"], 1)

            def stats(src, n):
                for t in range(NT):
                    last = v.bn_stats(stat[:, t], src[:, t])
                last.then_inc(s["st_x"], 1)
                dve.wait_ge(s["st_x"], n)
                for t in range(NT):
                    last = v.bn_aggr(mv[:, t], stat[:, t])
                last.then_inc(s["agg_x"], 1)
                dve.wait_ge(s["agg_x"], n)

            stats(x_all, 1)
            v.tensor_scalar_add(ve[:, :], mv[:, :, 1], EPS).then_inc(s["ve_x"], 1)
            for p in (0, 1):
                v.memset(vaug[:, p], 0.0).then_inc(s["vmem"], 1)
            dve.wait_ge(s["vmem"], 2)
            for p in (0, 1):
                v.memset(vaug[:, p, :, :, DH:DH + 1], 1.0)
            dve.wait_ge(s["rs_x"], 1)

            def normalise_x(b):
                p = b.parity
                if b.follows(2):
                    dve.wait_ge(s["xnT_r"], b.times(1, -1))
                for t in (0, 1):
                    if b.trip is None:
                        n = 2 * b.k + t
                        src, mean, r = x_all[:, n], mv[:, n, 0:1], rstd[:, n:n + 1]
                    else:
                        n = b.times(2, t)
                        src = x_all[:, bass.ds(n, 1), :].rearrange("p o d -> p (o d)")
                        mean = mv[:, bass.ds(n, 1), 0]
                        r = rstd[:, bass.ds(n, 1)]
                    last = v.tensor_scalar(xn[:, p, t], src, mean, r, ALU.subtract, ALU.mult)
                last.then_inc(s["xn_r"], 1)

            def residue(b):
                p = b.parity
                dve.wait_ge(s["hi_d"], b.times(1, 1))
                if b.follows(1):
                    dve.wait_ge(s["parts_d"], b.times(1))
                v.tensor_tensor(res1[:, :], M[:, :], qkp[:, p, 0].rearrange("p s t -> p (s t)"),
                                ALU.subtract).then_inc(s["r1_d"], 1)

            def values(b):
                p = b.parity
                dve.wait_ge(s["v_r"], b.times(1, 1))
                if b.follows(2):
                    dve.wait_ge(s["pv"], b.times(NG, -NG))
                v.tensor_copy(vaug[:, p, :, :, 0:DH], M[:, 0:SEQ].rearrange("p (t h d) -> p t h d", t=2, d=DH)).then_inc(s["v_d"], 1)

            def maxima(b, gr):
                p = b.parity
                for u in range(3):
                    n = 3 * gr + u
                    dve.wait_ge(s["s_r"], b.times(12, n + 1))
                    if u == 0:
                        dst, k = nmf[:, p, 4 * gr:4 * gr + 4, 0], 4
                    else:
                        dst, k = nmf[:, p, 4 * gr + 2 * (u - 1):4 * gr + 2 * u, 1], 2
                    v.tensor_reduce(dst, S[:, n % 2].rearrange("p (j n) -> p j n", j=k), op=ALU.max, axis=AX_X,
                                    negate=True).then_inc(s["red"], 1)
                if gr % 2:
                    half = gr // 2
                    src = nmf[:, p, 8 * half:8 * half + 8].rearrange("p h q -> p (h q)")
                    dve.wait_ge(s["red"], b.times(12, 3 * gr + 3))
                    if b.follows(2):
                        dve.wait_ge(s["shT_r"], b.times(2, half - 3))
                    v.tensor_copy(nmp[:, p, half, 0], src).then_inc(s["nm_hi"], 1)
                    dve.wait_ge(s["nm_hi"], b.times(2, half + 1))
                    v.tensor_tensor(nmp[:, p, half, 1], src, nmp[:, p, half, 0], ALU.subtract).then_inc(s["nm_d"], 1)

            def divide(i, qb):
                mo = M[:, :].rearrange("p (h n) -> p h n", n=32)
                dve.wait_ge(s["otr_r"], i.times(2, qb + 1))
                v.reciprocal(rden[:, qb], mo[:, :, DH]).then_inc(s["rden_d"], 1)
                dve.wait_ge(s["rden_d"], i.times(2, qb + 1))
                if i.follows(1):
                    dve.wait_ge(s["onT_r"], i.times(1))
                v.tensor_tensor(on[:, qb], mo[:, :, 0:DH], rden[:, qb].unsqueeze(2).to_broadcast([P, NH, DH]), ALU.mult).then_inc(s["on_d"], 1)

            def output(i):
                dve.wait_ge(s["y_r"], i.times(1, 1))
                if i.trip is None:
                    dst = y_all[:, 2 * i.k:2 * i.k + 2]
                else:
                    dst = y_all[:, bass.ds(i.times(2), 2), :]
                v.tensor_copy(dst, M[:, 0:SEQ].rearrange("p (t n) -> p t n", t=2)).then_inc(s["y_d"], 1)

            normalise_x(Batch(0))
            normalise_x(Batch(1))
            residue(Batch(0))
            values(Batch(0))
            residue(Batch(1))
            for gr in range(NG):
                maxima(Batch(0), gr)

            def step(i):
                if i.k + 2 <= LAST:
                    normalise_x(i.plus(2))
                if i.k + 1 <= LAST:
                    maxima(i.plus(1), 0)
                if i.k >= 1:
                    divide(i.plus(-1), 0)
                if i.k + 1 <= LAST:
                    maxima(i.plus(1), 1)
                if i.k + 2 <= LAST:
                    residue(i.plus(2))
                if i.k >= 1:
                    divide(i.plus(-1), 1)
                if i.k + 1 <= LAST:
                    maxima(i.plus(1), 2)
                    values(i.plus(1))
                    maxima(i.plus(1), 3)
                if i.k >= 1:
                    output(i.plus(-1))

            iterations(dve, step)

            chain = [0]

            def link(ins):
                chain[0] += 1
                ins.then_inc(s["tl"], 1)
                dve.wait_ge(s["tl"], chain[0])

            def normalise(dst, src):
                for t in range(NT):
                    last = v.tensor_scalar(dst(t), src[:, t], mv[:, t, 0:1], rstd[:, t:t + 1], ALU.subtract, ALU.mult)
                return last

            dve.wait_ge(s["y_d"], B)
            stats(y_all, 2)
            v.tensor_scalar_add(ve[:, :], mv[:, :, 1], EPS).then_inc(s["lnc"], 1)
            dve.wait_ge(s["rs_b"], 1)
            dve.wait_ge(s["zero_w"], 16)
            link(normalise(lambda t: f_all[:, t], y_all))
            link(v.tensor_tensor(x_all[:, :, :], x_all[:, :, :], f_all[:, :, :], ALU.add))
            stats(x_all, 3)
            v.tensor_scalar_add(ve[:, :], mv[:, :, 1], EPS).then_inc(s["lnc"], 1)
            dve.wait_ge(s["rs_b"], 2)
            link(normalise(lambda t: f_all[:, t], x_all))
            stats(f_all, 4)
            v.tensor_scalar_add(ve[:, :], mv[:, :, 1], EPS).then_inc(s["lnc"], 1)
            dve.wait_ge(s["rs_b"], 3)
            normalise(lambda t: pay[:, t, 0:D], f_all)
            dve.wait_ge(s["ids"], 1)
            link(v.tensor_copy(pay[:, :, D:ROW].bitcast(I32).rearrange("p t o -> p (t o)"), tokid[:, :]))
            dve.wait_ge(s["aff_r"], NT // 4)
            dve.wait_ge(s["consts"], 8)
            link(v.tensor_copy(aff[:, :, :], M[:, 0:NT * E].rearrange("p (t e) -> p t e", e=E)))
            link(v.tensor_reduce(amax[:, :], aff[:, :, :], op=ALU.max, axis=AX_X))
            by_t = amax[:, :].unsqueeze(2).to_broadcast([P, NT, E])
            link(v.tensor_tensor(hot[:, :, :], aff[:, :, :], by_t, ALU.is_equal))
            link(v.tensor_tensor(hot[:, :, :], hot[:, :, :], down[:, :].unsqueeze(1).to_broadcast([P, NT, E]), ALU.mult))
            link(v.tensor_reduce(key[:, :], hot[:, :, :], op=ALU.max, axis=AX_X))
            link(v.tensor_tensor(hot[:, :, :], hot[:, :, :], key[:, :].unsqueeze(2).to_broadcast([P, NT, E]), ALU.is_equal))
            v.tensor_copy(hotb[:, :, :], hot[:, :, :]).then_inc(s["hot_d"], 1)
            dve.wait_ge(s["cnt_r"], 1)
            v.tensor_copy(base[:, :, :], M[:, 0:NT * E].rearrange("p (t e) -> p t e", e=E))
            link(v.tensor_copy(cnt[:, 0], M[:, NT * E:2 * NT * E].rearrange("p (t e) -> p t e", e=E)))
            link(v.tensor_tensor(base[:, :, :], base[:, :, :], cnt[:, 0], ALU.subtract))
            cur, n = 0, 1
            while n < NT:
                v.tensor_copy(cnt[:, 1 - cur, 0:n], cnt[:, cur, 0:n])
                link(v.tensor_tensor(cnt[:, 1 - cur, n:NT], cnt[:, cur, n:NT], cnt[:, cur, 0:NT - n], ALU.add))
                cur, n = 1 - cur, 2 * n
            link(v.tensor_tensor(base[:, :, :], base[:, :, :], cnt[:, cur], ALU.add))
            link(v.tensor_tensor(above[:, :, :], cnt[:, cur, NT - 1].unsqueeze(2).to_broadcast([P, E, NT]),
                                 steps[:, :].unsqueeze(1).to_broadcast([P, E, NT]), ALU.is_gt))
            link(v.tensor_reduce(ntile[:, 0], above[:, :, :], op=ALU.add, axis=AX_X))
            tcur, n = 0, 1
            while n < E:
                v.tensor_copy(ntile[:, tcur + 1, 0:n], ntile[:, tcur, 0:n])
                link(v.tensor_tensor(ntile[:, tcur + 1, n:E], ntile[:, tcur, n:E], ntile[:, tcur, 0:E - n], ALU.add))
                tcur, n = tcur + 1, 2 * n
            link(v.tensor_tensor(tstart[:, :], ntile[:, tcur], ntile[:, 0], ALU.subtract))
            link(v.tensor_scalar(tstart[:, :], tstart[:, :], float(P), None, ALU.mult))
            link(v.tensor_tensor(over[:, :, :], slots[:, :].unsqueeze(2).to_broadcast([P, ST, E]),
                                 ntile[:, tcur].unsqueeze(1).to_broadcast([P, ST, E]), ALU.is_ge))
            link(v.tensor_reduce(esel[:, :], over[:, :, :], op=ALU.add, axis=AX_X))
            link(v.tensor_scalar(esel[:, :], esel[:, :], float(E - 1), None, ALU.min))
            v.tensor_copy(eidx[:, :], esel[:, :]).then_inc(s["rt"], 1)
            link(v.tensor_tensor(base[:, :, :], base[:, :, :], tstart[:, :].unsqueeze(1).to_broadcast([P, NT, E]), ALU.add))
            link(v.tensor_tensor(base[:, :, :], base[:, :, :], hot[:, :, :], ALU.mult))
            link(v.tensor_reduce(posf[:, :], base[:, :, :], op=ALU.add, axis=AX_X))
            v.tensor_copy(pos[:, :], posf[:, :]).then_inc(s["pos_d"], 1)
            dve.wait_ge(s["ex_d"], 1)
            link(v.tensor_scalar_add(eneg[:, :], eneg[:, :], 1.0))
            link(v.reciprocal(alpha[:, :], eneg[:, :]))
            dve.wait_ge(s["rt"], 1)
            dve.wait_ge(s["w_ffn"], 16 * (E + 5))

            def tile_in(t, p, first):
                e = dve.value_load(eidx[0:1, bass.ds(t * 2 + p, 1)], min_val=0, max_val=E - 1)
                if not first:
                    dve.wait_ge(s["ha_d"], t * 2 + (p - 1))
                    dve.wait_ge(s["h_r"], t * 4 + (2 * p - 2))
                    dve.wait_ge(s["hd_d"], t * 2 + (p - 1))
                v.tensor_copy(w1s[:, p], w1_tab[:, bass.ds(e, 1), :].rearrange("p o n -> p (o n)")).then_inc(s["w1_d"], 1)
                return e

            def tile_mid(t, p, first):
                dve.wait_ge(s["h_r"], t * 4 + (2 * p + 2))
                dve.wait_ge(s["w1_d"], t * 2 + (p + 1))
                if not first:
                    dve.wait_ge(s["z_r"], t * 2 + (p - 1))
                for c in range(FC // 2, FC):
                    last = v.tensor_scalar(hs[:, p, c], hidden(p, c), w1s[:, p, F + 2 + c:F + 3 + c], 0.0,
                                           ALU.add, ALU.max)
                last.then_inc(s["hd_d"], 1)

            def tile_out(t, p, e, first):
                dve.wait_ge(s["z_r"], t * 2 + (p + 1))
                if not first:
                    dve.wait_ge(z_sc[p], t * 16)
                v.tensor_tensor(zo[:, p], O[:, p, 0, 0:D], b2_tab[:, bass.ds(e * D, D)], ALU.add).then_inc(s["zo_d"], 1)

            def pair(t, first):
                e0 = tile_in(t, 0, first)
                e1 = tile_in(t, 1, first)
                tile_mid(t, 0, first)
                tile_mid(t, 1, first)
                tile_out(t, 0, e0, first)
                tile_out(t, 1, e1, first)

            pair(0, True)
            with dve.Fori(1, ST // 2) as t:
                pair(t, False)

            dve.wait_ge(s["z_in"], 16)
            for t in range(NT):
                last = v.scalar_tensor_tensor(out=y_all[:, t], in0=y_all[:, t], scalar=alpha[:, t:t + 1], in1=f_all[:, t],
                                              op0=ALU.mult, op1=ALU.add)
            link(last)
            stats(y_all, 5)
            v.tensor_scalar_add(ve[:, :], mv[:, :, 1], EPS).then_inc(s["lnc"], 1)
            dve.wait_ge(s["rs_b"], 4)
            link(normalise(lambda t: f_all[:, t], y_all))
            with dve.Fori(0, NT // 4) as c:
                v.tensor_tensor(x_all[:, bass.ds(c * 4, 4), :], x_all[:, bass.ds(c * 4, 4), :],
                                f_all[:, bass.ds(c * 4, 4), :], ALU.add).then_inc(s["out_w"], 1)


def kernel(L0_attn_x, L0_attn_WQ, L0_attn_WK, L0_attn_WV, L0_attn_WO, L0_ffn_centroids, L0_ffn_ln_g, L0_ffn_ln_b,
           L0_ffn_w1, L0_ffn_b1, L0_ffn_w2, L0_ffn_b2):
    import concourse.bacc as bacc
    from concourse.bass_utils import run_bass_kernel_spmd

    nh, dh, d = L0_attn_WQ.shape
    e, f, _ = L0_ffn_w1.shape
    attn_w = np.stack([np.asarray(w).reshape(nh * dh, d).T for w in (L0_attn_WQ, L0_attn_WK, L0_attn_WV)]
                      + [np.asarray(L0_attn_WO).transpose(0, 2, 1).reshape(nh * dh, d)])
    w1t = np.asarray(L0_ffn_w1).transpose(0, 2, 1)
    w2t = np.asarray(L0_ffn_w2).reshape(e, d, f // 128, 128).transpose(3, 0, 2, 1).reshape(128, -1)
    ln_cols = np.stack([np.asarray(L0_ffn_ln_g), np.asarray(L0_ffn_ln_b)], axis=-1).transpose(1, 0, 2)
    b1_cols = np.asarray(L0_ffn_b1).reshape(e, f // 128, 128).transpose(2, 0, 1)
    arrays = {"x": L0_attn_x, "attn_w": attn_w, "w1t": w1t, "w2t": w2t, "ln_cols": ln_cols, "b1_cols": b1_cols,
              "b2": L0_ffn_b2, "cent_t": np.asarray(L0_ffn_centroids).T}
    nc = bacc.Bacc("TRN2", target_bir_lowering=False, num_devices=1)
    ins, args = {}, {}
    for name, value in arrays.items():
        value = np.ascontiguousarray(value)
        ins[f"in_{name}"] = value
        args[name] = nc.dram_tensor(f"in_{name}", value.shape, mybir.dt.from_np(value.dtype), kind="ExternalInput").ap()
    out = nc.dram_tensor("out_x", tuple(L0_attn_x.shape), F32, kind="ExternalOutput").ap()
    sandwich_kernel(nc, out=out, **args)
    return run_bass_kernel_spmd(nc, [ins], core_ids=[0]).results[0]["out_x"]
```

```python
from contextlib import ExitStack

import numpy as np

import concourse.bass as bass
from concourse import mybir

ALU = mybir.AluOpType
ACT = mybir.ActivationFunctionType
AX_X = mybir.AxisListType.X
F32 = mybir.dt.float32
BF16 = mybir.dt.bfloat16
I32 = mybir.dt.int32
U32 = mybir.dt.uint32

P = 128
EPS = 1e-5
NEG = -1e30


class Nth:

    def __init__(self, k, trip=None, unroll=1):
        self.k, self.trip, self.unroll = k, trip, unroll

    def plus(self, n):
        return Nth(self.k + n, self.trip, self.unroll)

    def times(self, a, b=0):
        return a * self.k + b if self.trip is None else self.trip * (self.unroll * a) + (a * self.k + b)

    def turns(self, ring, a, b=0):
        here = a * (self.k // ring) + b
        return here if self.trip is None else self.trip * (self.unroll // ring * a) + here

    def slot(self, ring):
        assert self.trip is None or self.unroll % ring == 0
        return self.k % ring

    def follows(self, n):
        return self.k >= n

    def pick(self, table, width=1, step=1, b=0):
        at = self.times(step, b)
        if self.trip is None:
            return table[:, at:at + width]
        return table[:, bass.ds(at, width)]


def sandwich_kernel(nc, x, attn_w, w1t, w2t, ln_cols, b1_cols, b2, cent_t, out):
    B, SEQ, D = x.shape
    NH = 16
    DH = D // NH
    E, _, F = w1t.shape
    NT = B * SEQ // P
    FC = F // P
    NG = NH // 4
    SCALE = float(DH) ** -0.5
    ST = NT + E
    ROW = D + 1
    SP1 = F + 2 + FC
    assert D == P and SEQ == 2 * P and B % 2 == 0

    RING = 3
    UB, UT = 3, 4
    NPAIR = 6
    SHIFT = P - 2

    xs_dram = nc.dram_tensor("xs_rows", (ST * P, ROW), F32, kind="Internal").ap()
    z_dram = nc.dram_tensor("z_rows", (NT * P + ST * P, D), F32, kind="Internal").ap()
    qk_dram = nc.dram_tensor("qk_parts", (RING, 2, 3, DH, NH, SEQ), BF16, kind="Internal").ap()
    sh_dram = nc.dram_tensor("shift_rows", (RING, 2, 2, 8 * SEQ), BF16, kind="Internal").ap()

    with ExitStack() as ctx:
        def sb(name, shape, dt=F32):
            return ctx.enter_context(nc.sbuf_tensor(name, shape, dt))

        def ps(name, shape, dt=F32):
            return ctx.enter_context(nc.psum_tensor(name, shape, dt))

        def sem(name):
            return ctx.enter_context(nc.semaphore(name))

        wat = sb("wat", [P, 4, D])
        w1_tab = sb("w1_tab", [P, E, SP1])
        w2_tab = sb("w2_tab", [P, E * FC * D])
        b2_tab = sb("b2_tab", [P, E * D])
        cent = sb("cent", [P, E])
        ident = sb("ident", [P, P])
        identb = sb("identb", [P, P], BF16)
        causal = sb("causal", [P, 4, P], BF16)
        before = sb("before", [P, P], BF16)
        onesb = sb("onesb", [P, P], BF16)
        mhalf = sb("mhalf", [P, NT])
        x_all = sb("x_all", [P, NT, D])
        late = sb("late", [P, NT * (D + ROW)])
        f_all = late[:, 0:NT * D].rearrange("p (t d) -> p t d", d=D)
        pay = late[:, NT * D:].rearrange("p (t d) -> p t d", d=ROW)
        fill = late[:, 0:ST * ROW].rearrange("p (t d) -> p t d", d=ROW)
        mvx = sb("mvx", [P, NT, 2])
        vex = sb("vex", [P, NT])
        rsx = sb("rsx", [P, NT])
        stx = sb("stx", [P, NT, 6])
        xn = sb("xn", [P, RING, 2, D])
        xnT = sb("xnT", [P, RING, SEQ])
        qkp = sb("qkp", [P, RING, 6, SEQ], BF16)
        res1 = sb("res1", [P, 2, SEQ])
        aug = sb("aug", [P, 2 * RING * NH * SEQ], BF16)
        augv = aug[:, :].rearrange("p (s r h t) -> p s r h t", s=2, r=RING, h=NH)
        qaug, kaug = augv[:, 0], augv[:, 1]
        nmf = sb("nmf", [P, RING, NH, 2])
        nmp = sb("nmp", [P, RING, 2, 2, 16], BF16)
        nmT = sb("nmT", [32, RING, 2, P], BF16)
        vaug = sb("vaug", [P, RING, 2, NH, 32])
        p0 = sb("p0", [P, 2, 4, SEQ])
        p1 = sb("p1", [P, 2, 4, P])
        oT = sb("oT", [P, 4, SEQ])
        rden = sb("rden", [P, 2, NH])
        on = sb("on", [P, 2, NH, DH])
        onT = sb("onT", [P, SEQ])
        yb = sb("yb", [P, RING, 2, D])
        yn = sb("yn", [P, 2, D])
        fb = sb("fb", [P, 2, D])
        st_ln = sb("st_ln", [P, 3, 2, 6])
        mv_ln = sb("mv_ln", [P, 3, 2, 2])
        ve_ln = sb("ve_ln", [P, 3, 2])
        rs_ln = sb("rs_ln", [P, 3, 2])
        fT = sb("fT", [P, 2, P])
        aff = sb("aff", [P, NT, E])
        amax = sb("amax", [P, NT])
        alpha = sb("alpha", [P, NT])
        eneg = sb("eneg", [P, NT])
        key = sb("key", [P, NT])
        down = sb("down", [P, E])
        steps = sb("steps", [P, NT])
        slots = sb("slots", [P, ST])
        ntile = sb("ntile", [P, 4, E])
        tstart = sb("tstart", [P, E])
        esel = sb("esel", [P, ST])
        eidx = sb("eidx", [P, ST], I32)
        posf = sb("posf", [P, NT])
        pos = sb("pos", [P, NT], I32)
        tokid = sb("tokid", [P, NT], I32)
        dumpid = sb("dumpid", [P, ST], I32)
        def carve(table, *shapes):
            flat = table[:].rearrange("p a b c d -> p (a b c d)" if len(table.shape) == 5 else
                                      "p a b c -> p (a b c)" if len(table.shape) == 4 else "p a b -> p (a b)")
            at, views = 0, []
            for shape in shapes:
                n = int(np.prod(shape))
                view = flat[:, at:at + n]
                if len(shape) == 2:
                    view = view.rearrange("p (a b) -> p a b", b=shape[1])
                if len(shape) == 3:
                    view = view.rearrange("p (a b c) -> p a b c", b=shape[1], c=shape[2])
                views.append(view)
                at += n
            return views

        hot, base, cnt, above, over = carve(p0, (NT, E), (NT, E), (2, NT, E), (E, NT), (ST, E))
        (hot_words,) = carve(p1, (NT * E // 2,))
        hotb = hot_words.bitcast(BF16).rearrange("p (t e) -> p t e", e=E)
        xs, w1s, nT, hs = carve(vaug, (4, ROW), (2, SP1), (2, P), (2, FC, P))
        (zo,) = carve(oT, (4, D))
        ids = sb("ids", [P, 4], I32)
        z_all = aug[:, 0:2 * NT * D].bitcast(F32).rearrange("p (t d) -> p t d", d=D)
        mvz = sb("mvz", [P, NT, 2])
        stz = sb("stz", [P, NT, 6])
        vez = sb("vez", [P, NT])
        rsz = sb("rsz", [P, NT])
        nbz = sb("nbz", [P, NT])

        S = ps("S", [P, 2, 512])
        ST0 = ps("ST0", [P, 4, SEQ])
        ST1 = ps("ST1", [P, 4, P])
        O = ps("O", [P, 2, 2, SEQ])
        M = ps("M", [P, 512])

        names = ("w_attn w_cent w_ffn x_in x_rest qzero kone zero_w ids_r consts pmem dmem vmem vones "
                 "st_x agg_x ve_x rs_x xn_r xnT_r xnT_d qk_r hi_d r1_d mid_d parts_d "
                 "v_r v_d s_r red nm_hi nm_d shT_r sh_d st0_r st1_r exp0 exp1 sel0 sel1 pv o_ev "
                 "otr_r rden_d on_d onT_r onT_d y_r y_d "
                 "ln_st ln_ag ln_ve ln_rs yn_d x2_d f_d fc_d pay_d fT_r fT_d aff_r aff_d id_in "
                 "ex_d hot_d cnt_r rt pos_d scat w1_d id_d xsT_r nT_d h_r ha_d hd_d z_r zo_d "
                 "zf_d st_z agg_z ve_z rs_z nb_z zn_d out_w tl").split()
        s = {n: sem(n) for n in names}
        qk_w = [sem(f"qk_w{p}") for p in range(RING)]
        aug_in = [sem(f"aug_in{p}") for p in range(RING)]
        sh_w = [sem(f"sh_w{h}") for h in (0, 1)]
        sh_in = [sem(f"sh_in{h}") for h in (0, 1)]
        xs_in = [sem(f"xs_in{p}") for p in range(4)]
        z_sc = [sem(f"z_sc{p}") for p in range(4)]
        z_in = [sem(f"z_in{c}") for c in range(NT // 4)]
        out_s = sem("out_s")

        block = ctx.enter_context(nc.Block())
        LAST = B - 1

        def part(p, c):
            return qkp[:, p, c:6 - c:5 - 2 * c, :]

        def hidden(p, c):
            return S[:, p, c * P:(c + 1) * P] if c < FC // 2 else ST0[:, 2 * p:2 * p + 2].rearrange("p a n -> p (a n)")[
                :, (c - FC // 2) * P:(c - FC // 2 + 1) * P]

        def wait_fixed(eng, name, value):
            if not isinstance(value, int):
                value = eng.compute_val(value)
            eng.wait_ge(s["consts"], 1)
            eng.wait_ge(name, value)

        def iterations(eng, step):
            first = UB + 1
            trips = (B - 3 - first) // UB
            for i in range(first):
                step(Nth(i))
            with eng.Fori(0, trips) as trip:
                for k in range(UB):
                    step(Nth(first + k, trip, UB))
            for i in range(first + trips * UB, B + 3):
                step(Nth(i))

        def tiles(eng, step):
            for k in range(-2, UT):
                step(Nth(k))
            with eng.Fori(0, ST // UT - 2) as trip:
                for k in range(UT):
                    step(Nth(UT + k, trip, UT))
            for k in range(ST - UT, ST):
                step(Nth(k))

        def at(i, stage):
            b = i.plus(stage)
            return b if 0 <= b.k <= LAST else None

        @block.sync
        def _(sp):
            xv = x.rearrange("b (t p) d -> p (b t) d", p=P)
            sp.dma_start(x_all[:, 0:2 * RING, :], xv[:, 0:2 * RING, :]).then_inc(s["x_in"], 16)
            sp.dma_start(wat[:, :, :], attn_w.rearrange("k p n -> p k n")).then_inc(s["w_attn"], 16)
            sp.dma_start(x_all[:, 2 * RING:NT, :], xv[:, 2 * RING:NT, :]).then_inc(s["x_rest"], 16)

            def parts_out(b):
                p = b.slot(RING)
                wait_fixed(sp, s["parts_d"], b.times(1, 1))
                if b.follows(RING):
                    wait_fixed(sp, aug_in[p], b.turns(RING, 96))
                sp.dma_start(qk_dram[p].rearrange("s c d h t -> (d h) (s c) t"), qkp[:, p]).then_inc(qk_w[p], 16)

            def parts_in(b):
                p = b.slot(RING)
                wait_fixed(sp, qk_w[p], b.turns(RING, 16, 16))
                if b.follows(RING):
                    wait_fixed(sp, s["st1_r"], b.times(NG, -NG * (RING - 1)))
                row = 0
                for n in (3, 2, 1):
                    rows = n * DH
                    sp.dma_start(qaug[row:row + rows, p], qk_dram[p, 0, 0:n].rearrange("c d h t -> (c d) h t"))\
                        .then_inc(aug_in[p], 16)
                    sp.dma_start(kaug[row:row + rows, p], qk_dram[p, 1, 3 - n:3].rearrange("c d h t -> (c d) h t"))\
                        .then_inc(aug_in[p], 16)
                    row += rows

            def shift(b, half):
                p = b.slot(RING)
                wait_fixed(sp, s["sh_d"], b.times(2, half + 1))
                if b.follows(RING):
                    wait_fixed(sp, sh_in[half], b.times(16, -16 * (RING - 1)))
                sp.dma_start(sh_dram[p, half].rearrange("c (r t) -> (c r) t", t=P), nmT[:, p, half])\
                    .then_inc(sh_w[half], 16)
                wait_fixed(sp, sh_w[half], b.times(16, 16))
                if b.follows(RING):
                    wait_fixed(sp, s["st1_r"], b.times(NG, -NG * (RING - 1)))
                sp.dma_start(qaug[SHIFT:P, p, 8 * half:8 * half + 8],
                             sh_dram[p, half].rearrange("c (h t) -> c h t", t=SEQ)).then_inc(sh_in[half], 16)

            parts_out(Nth(0))
            sp.wait_ge(s["qzero"], 1)
            sp.wait_ge(s["kone"], 1)
            parts_in(Nth(0))
            parts_out(Nth(1))
            sp.wait_ge(s["qzero"], 3)
            sp.wait_ge(s["kone"], 3)
            parts_in(Nth(1))
            shift(Nth(0), 0)

            def step(i):
                if b := at(i, 2):
                    parts_out(b)
                if b := at(i, 0):
                    shift(b, 1)
                if b := at(i, 2):
                    parts_in(b)
                if b := at(i, 1):
                    shift(b, 0)
                if i.trip is None and i.k <= B:
                    e = i.k if i.k <= UB else i.k - (B + 1 - E)
                    sp.dma_start(w1_tab[:, e, 0:F], w1t[e]).then_inc(s["w_ffn"], 16)
                    sp.dma_start(w2_tab[:, e * FC * D:(e + 1) * FC * D], w2t[:, e * FC * D:(e + 1) * FC * D])\
                        .then_inc(s["w_ffn"], 16)
                if i.k == 0:
                    sp.dma_start(cent[:, :], cent_t).then_inc(s["w_cent"], 16)
                    sp.dma_start(w1_tab[:, :, F:F + 2], ln_cols).then_inc(s["w_ffn"], 16)
                    sp.dma_start(w1_tab[:, :, F + 2:SP1], b1_cols).then_inc(s["w_ffn"], 16)
                    sp.dma_start(b2_tab[:, :], b2.rearrange("(o e) d -> o (e d)", o=1).to_broadcast([P, E * D]))\
                        .then_inc(s["w_ffn"], 16)
                if i.k == 1:
                    sp.wait_ge(s["ids_r"], 3)
                    sp.dma_start(xs_dram.rearrange("(t p) d -> p t d", p=P), fill[:, :, :]).then_inc(s["zero_w"], 16)

            iterations(sp, step)

            sp.wait_ge(s["scat"], 16 * NT)

            def rows_in(t):
                p = t.slot(4)
                if t.follows(4):
                    wait_fixed(sp, s["id_d"], t.times(1, -3))
                    wait_fixed(sp, s["xsT_r"], t.times(1, -3))
                if t.trip is None:
                    src = xs_dram[t.k * P:(t.k + 1) * P, :]
                else:
                    src = xs_dram[bass.ds(t.times(P), P), :]
                sp.dma_start(xs[:, p], src).then_inc(xs_in[p], 16)

            for t in range(UT):
                rows_in(Nth(t))
            with sp.Fori(0, ST // UT - 1) as trip:
                for k in range(UT):
                    rows_in(Nth(UT + k, trip, UT))
            for p in range(4):
                sp.wait_ge(z_sc[p], 4 * ST)
            for c in range(NT // 4):
                sp.dma_start(z_all[:, 4 * c:4 * c + 4, :],
                             z_dram[4 * c * P:4 * (c + 1) * P, :].rearrange("(t p) d -> p t d", p=P)).then_inc(z_in[c], 16)
            ov = out.rearrange("b (t p) d -> p (b t) d", p=P)
            for c in range(NT // 4):
                sp.wait_ge(s["out_w"], c + 1)
                sp.dma_start(ov[:, 4 * c:4 * c + 4, :], x_all[:, 4 * c:4 * c + 4, :]).then_inc(out_s, 16)
            sp.wait_ge(out_s, 16 * (NT // 4))

        @block.gpsimd
        def _(pool):
            g = nc.gpsimd
            two_ones = float(np.array([0x3F803F80], np.uint32).view(np.float32)[0])
            g.memset(ident[:, :], 0.0).then_inc(s["pmem"], 1)
            g.memset(mhalf[:, :], -0.5).then_inc(s["consts"], 1)
            pool.wait_ge(s["pmem"], 1)
            g.affine_select(out=ident[:, :], in_=ident[:, :], compare_op=ALU.not_equal, fill=1.0, base=0,
                            pattern=[[-1, P]], channel_multiplier=1).then_inc(s["consts"], 1)
            pool.wait_ge(s["consts"], 2)
            pool.wait_ge(s["ve_x"], 1)
            g.tensor_tensor(rsx[:, 0:2 * RING], vex[:, 0:2 * RING], mhalf[:, 0:2 * RING], op=ALU.pow).then_inc(s["rs_x"], 1)
            g.memset(kaug[:, 0].bitcast(F32), two_ones).then_inc(s["kone"], 1)
            g.memset(causal[:, :, :], 0.0).then_inc(s["pmem"], 1)
            g.memset(before[:, :], 1.0).then_inc(s["pmem"], 1)
            g.memset(onesb[:, :], 1.0).then_inc(s["consts"], 1)
            g.tensor_copy(identb[:, :], ident[:, :]).then_inc(s["consts"], 1)
            pool.wait_ge(s["pmem"], 3)
            g.affine_select(out=causal[:, :, :], in_=causal[:, :, :], compare_op=ALU.is_ge, fill=NEG, base=0,
                            pattern=[[0, 4], [-1, P]], channel_multiplier=1).then_inc(s["consts"], 1)
            g.affine_select(out=before[:, :], in_=before[:, :], compare_op=ALU.is_gt, fill=0.0, base=0,
                            pattern=[[1, P]], channel_multiplier=-1).then_inc(s["consts"], 1)

            def low(b):
                p = b.slot(RING)
                pool.wait_ge(s["mid_d"], b.times(1, 1))
                if b.follows(RING):
                    pool.wait_ge(qk_w[p], b.turns(RING, 16))
                g.tensor_tensor(part(p, 2), res1[:, :, :], part(p, 1), op=ALU.subtract).then_inc(s["parts_d"], 1)

            def select(i, gr):
                v = p0[:, gr % 2, :, 0:P]
                wait_fixed(pool, s["exp0"], i.times(NG, gr + 1))
                g.affine_select(out=v, in_=v, compare_op=ALU.is_ge, fill=0.0, base=0,
                                pattern=[[0, 4], [1, P]], channel_multiplier=-1).then_inc(s["sel0"], 1)
                wait_fixed(pool, s["exp1"], i.times(NG, gr + 1))
                v = p1[:, gr % 2]
                g.affine_select(out=v, in_=v, compare_op=ALU.is_ge, fill=0.0, base=0,
                                pattern=[[0, 4], [1, P]], channel_multiplier=-1).then_inc(s["sel1"], 1)

            def power(b, n):
                pool.wait_ge(s["ln_ve"], b.times(3, n + 1))
                g.tensor_tensor(rs_ln[:, n], ve_ln[:, n], mhalf[:, 0:2], op=ALU.pow).then_inc(s["ln_rs"], 1)

            low(Nth(0))
            g.memset(kaug[:, 1].bitcast(F32), two_ones).then_inc(s["kone"], 1)
            g.memset(kaug[:, 2].bitcast(F32), two_ones).then_inc(s["kone"], 1)
            low(Nth(1))
            pool.wait_ge(s["ve_x"], 2)
            g.tensor_tensor(rsx[:, 2 * RING:NT], vex[:, 2 * RING:NT], mhalf[:, 2 * RING:NT], op=ALU.pow).then_inc(s["rs_x"], 1)
            g.iota(tokid[:, :], [[P, NT]], base=0, channel_multiplier=1).then_inc(s["ids_r"], 1)
            g.iota(dumpid[:, :], [[P, ST]], base=NT * P, channel_multiplier=1).then_inc(s["dmem"], 1)
            g.iota(down[:, :], [[-1, E]], base=E, channel_multiplier=0,
                   allow_small_or_imprecise_dtypes=True).then_inc(s["consts"], 1)
            g.iota(steps[:, :], [[P, NT]], base=0, channel_multiplier=0,
                   allow_small_or_imprecise_dtypes=True).then_inc(s["consts"], 1)
            g.iota(slots[:, :], [[1, ST]], base=0, channel_multiplier=0,
                   allow_small_or_imprecise_dtypes=True).then_inc(s["consts"], 1)
            g.memset(fill[:, :, 0:D], 0.0).then_inc(s["ids_r"], 1)
            pool.wait_ge(s["dmem"], 1)
            g.tensor_copy(fill[:, :, D:ROW].bitcast(I32).rearrange("p t o -> p (t o)"), dumpid[:, :]).then_inc(s["ids_r"], 1)
            low(Nth(2))

            def step(i):
                t, ln = at(i, 0), at(i, -2)
                if t:
                    select(t, 0)
                if t:
                    select(t, 1)
                if ln:
                    power(ln, 0)
                if t:
                    select(t, 2)
                if ln:
                    power(ln, 1)
                if t:
                    select(t, 3)
                if ln:
                    power(ln, 2)
                if b := at(i, 3):
                    low(b)
                if i.k == 3:
                    pool.wait_ge(s["zero_w"], 16)
                    pool.wait_ge(s["ids_r"], 1)
                    g.tensor_copy(pay[:, :, D:ROW].bitcast(I32).rearrange("p t o -> p (t o)"), tokid[:, :])\
                        .then_inc(s["id_in"], 1)

            iterations(pool, step)

            pool.wait_ge(s["pay_d"], B)
            pool.wait_ge(s["id_in"], 1)
            pool.wait_ge(s["pos_d"], 1)
            for t in range(NT):
                g.indirect_dma_start(out=xs_dram, out_offset=bass.IndirectOffsetOnAxis(ap=pos[:, t:t + 1].bitcast(U32), axis=0),
                                     in_=pay[:, t, :], in_offset=None).then_inc(s["scat"], 16)

            def rows_out(t):
                p = t.slot(4)
                wait_fixed(pool, s["zo_d"], t.times(1, 1))
                g.indirect_dma_start(out=z_dram, out_offset=bass.IndirectOffsetOnAxis(ap=ids[:, p:p + 1].bitcast(U32), axis=0),
                                     in_=zo[:, p, :], in_offset=None).then_inc(z_sc[p], 16)

            for t in range(UT):
                rows_out(Nth(t))
            with pool.Fori(0, ST // UT - 1) as trip:
                for k in range(UT):
                    rows_out(Nth(UT + k, trip, UT))
            for c in range(NT // 4):
                q = slice(4 * c, 4 * c + 4)
                pool.wait_ge(s["ve_z"], c + 1)
                g.tensor_tensor(rsz[:, q], vez[:, q], mhalf[:, 0:4], op=ALU.pow).then_inc(s["rs_z"], 1)
                if c >= 1:
                    q = slice(4 * c - 4, 4 * c)
                    pool.wait_ge(s["zn_d"], c)
                    g.tensor_tensor(x_all[:, q], x_all[:, q], f_all[:, q], op=ALU.add).then_inc(s["out_w"], 1)
            q = slice(NT - 4, NT)
            pool.wait_ge(s["zn_d"], NT // 4)
            g.tensor_tensor(x_all[:, q], x_all[:, q], f_all[:, q], op=ALU.add).then_inc(s["out_w"], 1)

        @block.scalar
        def _(act):
            a = nc.scalar

            def xnT_out(b):
                p = b.slot(RING)
                act.wait_ge(s["xnT_r"], b.times(1, 1))
                if b.follows(RING):
                    act.wait_ge(s["v_r"], b.times(1, 1 - RING))
                a.activation(xnT[:, p], M[:, 0:SEQ], ACT.Copy).then_inc(s["xnT_d"], 1)

            def high(b):
                p = b.slot(RING)
                act.wait_ge(s["qk_r"], b.times(1, 1))
                if b.follows(RING):
                    act.wait_ge(qk_w[p], b.turns(RING, 16))
                a.activation(part(p, 0), M[:, :].rearrange("p (s t) -> p s t", s=2), ACT.Copy).then_inc(s["hi_d"], 1)

            def middle(b):
                p = b.slot(RING)
                act.wait_ge(s["r1_d"], b.times(1, 1))
                a.activation(part(p, 1), res1[:, :, :], ACT.Copy).then_inc(s["mid_d"], 1)

            def shift_out(b, half):
                act.wait_ge(s["shT_r"], b.times(2, half + 1))
                if b.follows(RING):
                    act.wait_ge(sh_w[half], b.times(16, 16 * (1 - RING)))
                a.activation(nmT[:, b.slot(RING), half], M[:, 0:P // 2].bitcast(BF16)[0:32, 0:P], ACT.Copy).then_inc(s["sh_d"], 1)

            def v_out(b):
                p = b.slot(RING)
                act.wait_ge(s["v_r"], b.times(1, 1))
                if b.follows(RING):
                    act.wait_ge(s["pv"], b.times(NG, NG * (1 - RING)))
                else:
                    act.wait_ge(s["vones"], p + 1)
                a.activation(vaug[:, p, :, :, 0:DH], M[:, 0:SEQ].rearrange("p (t h d) -> p t h d", t=2, d=DH),
                             ACT.Copy).then_inc(s["v_d"], 1)

            def exp_near(i, gr):
                act.wait_ge(s["st0_r"], i.times(NG, gr + 1))
                if i.k > 0 or gr >= 2:
                    act.wait_ge(s["pv"], i.times(NG, gr - 1))
                a.activation(p0[:, gr % 2], ST0[:, :, :], ACT.Exp, scale=SCALE).then_inc(s["exp0"], 1)

            def exp_far(i, gr):
                act.wait_ge(s["st1_r"], i.times(NG, gr + 1))
                a.activation(p1[:, gr % 2], ST1[:, :, :], ACT.Exp, scale=SCALE).then_inc(s["exp1"], 1)

            def o_out(i, half):
                act.wait_ge(s["pv"], i.times(NG, 2 * half + 2))
                if i.follows(1):
                    act.wait_ge(s["otr_r"], i.times(2))
                a.activation(oT[:, 2 * half:2 * half + 2], O[:, half], ACT.Copy).then_inc(s["o_ev"], 1)

            def onT_out(i):
                act.wait_ge(s["onT_r"], i.times(1, 1))
                if i.follows(1):
                    act.wait_ge(s["y_r"], i.times(1))
                a.activation(onT[:, :], M[:, 0:SEQ], ACT.Copy).then_inc(s["onT_d"], 1)

            def y_out(i):
                act.wait_ge(s["y_r"], i.times(1, 1))
                if i.follows(RING):
                    act.wait_ge(s["yn_d"], i.times(1, 1 - RING))
                a.activation(yb[:, i.slot(RING)], M[:, 0:SEQ].rearrange("p (t d) -> p t d", t=2), ACT.Copy).then_inc(s["y_d"], 1)

            def f_copy(i):
                act.wait_ge(s["f_d"], i.times(1, 1))
                if i.k == 0:
                    act.wait_ge(s["zero_w"], 16)
                a.activation(i.pick(f_all, 2, 2), fb[:, :, :], ACT.Copy).then_inc(s["fc_d"], 1)

            def fT_out(i):
                act.wait_ge(s["fT_r"], i.times(1, 1))
                if i.follows(1):
                    act.wait_ge(s["aff_r"], i.times(1))
                a.activation(fT[:, :, :], M[:, 0:SEQ].rearrange("p (t n) -> p t n", t=2), ACT.Copy).then_inc(s["fT_d"], 1)

            def aff_out(i):
                act.wait_ge(s["aff_r"], i.times(1, 1))
                a.activation(i.pick(aff, 2, 2), M[:, 0:2 * E].rearrange("p (t e) -> p t e", e=E), ACT.Copy).then_inc(s["aff_d"], 1)

            for n in (0, 1):
                xnT_out(Nth(n))
                high(Nth(n))
                middle(Nth(n))
                if n == 0:
                    v_out(Nth(n))
            xnT_out(Nth(2))
            shift_out(Nth(0), 0)
            high(Nth(2))
            middle(Nth(2))

            def step(i):
                t, new, nxt, old, ln = at(i, 0), at(i, 3), at(i, 1), at(i, -1), at(i, -3)
                if t:
                    exp_near(t, 0)
                    shift_out(t, 1)
                    exp_far(t, 0)
                if old:
                    o_out(old, 1)
                if ln:
                    fT_out(ln)
                if t:
                    exp_near(t, 1)
                if ln:
                    f_copy(ln)
                if t:
                    exp_far(t, 1)
                if ln:
                    aff_out(ln)
                if t:
                    exp_near(t, 2)
                if nxt:
                    shift_out(nxt, 0)
                if t:
                    exp_far(t, 2)
                if new:
                    xnT_out(new)
                if t:
                    o_out(t, 0)
                if nxt:
                    v_out(nxt)
                if t:
                    exp_near(t, 3)
                if old:
                    onT_out(old)
                if t:
                    exp_far(t, 3)
                if old:
                    y_out(old)
                if new:
                    high(new)
                    middle(new)

            iterations(act, step)

            act.wait_ge(s["hot_d"], 1)
            a.activation(eneg[:, :], amax[:, :], ACT.Exp, scale=-1.0).then_inc(s["ex_d"], 1)

            def enter(t):
                p = t.slot(2)
                act.wait_ge(s["w1_d"], t.times(1, 1))
                act.wait_ge(s["xsT_r"], t.times(1, 1))
                if t.follows(2):
                    act.wait_ge(s["h_r"], t.times(2, -2))
                a.activation(nT[:, p], (M, ST1[:, 0])[p][:, 0:P], ACT.Identity, scale=w1s[:, p, F:F + 1],
                             bias=w1s[:, p, F + 1:F + 2]).then_inc(s["nT_d"], 1)

            def relu(t):
                p = t.slot(2)
                act.wait_ge(s["h_r"], t.times(2, 1))
                if t.follows(2):
                    act.wait_ge(s["z_r"], t.times(1, -1))
                for c in range(FC // 2):
                    last = a.activation(hs[:, p, c], hidden(p, c), ACT.Relu, bias=w1s[:, p, F + 2 + c:F + 3 + c])
                last.then_inc(s["ha_d"], 1)

            def tile_step(t):
                if t.k + 2 < ST:
                    enter(t.plus(2))
                if 0 <= t.k + 1 < ST:
                    relu(t.plus(1))

            tiles(act, tile_step)

            for c in range(NT // 4):
                act.wait_ge(s["nb_z"], c + 1)
                for t in range(4 * c, 4 * c + 4):
                    last = a.activation(f_all[:, t], z_all[:, t], ACT.Identity, scale=rsz[:, t:t + 1], bias=nbz[:, t:t + 1])
                last.then_inc(s["zn_d"], 1)

        @block.tensor
        def _(pe):
            mm = nc.tensor.matmul
            m_free = [[]]

            def take_m():
                for name, value in m_free[0]:
                    pe.wait_ge(s[name], value)

            def transpose_x(b):
                take_m()
                pe.wait_ge(s["xn_r"], b.times(1, 1))
                for t in (0, 1):
                    last = nc.tensor.transpose(M[:, t * P:(t + 1) * P], xn[:, b.slot(RING), t], ident[:, :])
                last.then_inc(s["xnT_r"], 1)
                m_free[0] = [("xnT_d", b.times(1, 1))]

            def project_qk(b):
                take_m()
                pe.wait_ge(s["xnT_d"], b.times(1, 1))
                for w in (0, 1):
                    last = mm(M[:, w * SEQ:(w + 1) * SEQ], wat[:, w], xnT[:, b.slot(RING)], start=True, stop=True)
                last.then_inc(s["qk_r"], 1)
                m_free[0] = [("hi_d", b.times(1, 1)), ("r1_d", b.times(1, 1))]

            def project_v(b):
                take_m()
                for t in (0, 1):
                    last = mm(M[:, t * P:(t + 1) * P], xnT[:, b.slot(RING), t * P:(t + 1) * P], wat[:, 2],
                              start=True, stop=True)
                last.then_inc(s["v_r"], 1)
                m_free[0] = [("v_d", b.times(1, 1))]

            def transpose_shift(b, half):
                take_m()
                pe.wait_ge(s["nm_d"], b.times(2, half + 1))
                nc.tensor.transpose(M[:, 0:P // 2].bitcast(BF16)[0:32, 0:P],
                                    nmp[:, b.slot(RING), half].rearrange("p c r -> p (c r)"), identb[:, :]).then_inc(s["shT_r"], 1)
                m_free[0] = [("sh_d", b.times(2, half + 1))]

            def scores_by_query(b, gr, u):
                p = b.slot(RING)
                n = 3 * gr + u
                if n == 0:
                    pe.wait_ge(aug_in[p], b.turns(RING, 96, 96))
                if b.k > 0 or n >= 2:
                    pe.wait_ge(s["red"], b.times(12, n - 1))
                bank = S[:, n % 2]
                q, k = qaug[0:SHIFT, p], kaug[0:SHIFT, p]
                if u == 0:
                    mm(bank, identb[:, :], causal[:, :, :], start=True, stop=False)
                    for j in range(4):
                        h = 4 * gr + j
                        last = mm(bank[:, j * P:(j + 1) * P], q[:, h, 0:P], k[:, h, 0:P], start=False, stop=(j == 3))
                else:
                    mm(bank.rearrange("p (j c n) -> p j c n", j=2, c=2)[:, :, 1], identb[:, :], causal[:, 0:2],
                       start=True, stop=False)
                    for j in range(2):
                        h = 4 * gr + 2 * (u - 1) + j
                        for kb in (0, 1):
                            last = mm(bank[:, j * SEQ + kb * P:j * SEQ + (kb + 1) * P], q[:, h, P:SEQ],
                                      k[:, h, kb * P:(kb + 1) * P], start=False, stop=(j == 1 and kb == 1))
                last.then_inc(s["s_r"], 1)

            def scores_near(i, gr):
                p = i.slot(RING)
                if gr % 2 == 0:
                    pe.wait_ge(sh_in[gr // 2], i.times(16, 16))
                if i.k > 0 or gr > 0:
                    pe.wait_ge(s["exp0"], i.times(NG, gr))
                for j in range(4):
                    h = 4 * gr + j
                    last = mm(ST0[:, j], kaug[:, p, h, 0:P], qaug[:, p, h], start=True, stop=True)
                last.then_inc(s["st0_r"], 1)

            def scores_far(i, gr):
                p = i.slot(RING)
                if i.k > 0 or gr > 0:
                    pe.wait_ge(s["exp1"], i.times(NG, gr))
                for j in range(4):
                    h = 4 * gr + j
                    last = mm(ST1[:, j], kaug[:, p, h, P:SEQ], qaug[:, p, h, P:SEQ], start=True, stop=True)
                last.then_inc(s["st1_r"], 1)

            def weigh_values(i, gr):
                p = i.slot(RING)
                if gr == 0:
                    pe.wait_ge(s["v_d"], i.times(1, 1))
                if i.k > 0 and gr % 2 == 0:
                    pe.wait_ge(s["o_ev"], i.times(2, gr // 2 - 1))
                pe.wait_ge(s["sel0"], i.times(NG, gr + 1))
                for j in range(4):
                    mm(O[32 * j:32 * j + 32, gr // 2, gr % 2, :], vaug[:, p, 0, 4 * gr + j], p0[:, gr % 2, j],
                       start=True, stop=False)
                pe.wait_ge(s["sel1"], i.times(NG, gr + 1))
                for j in range(4):
                    last = mm(O[32 * j:32 * j + 32, gr // 2, gr % 2, P:SEQ], vaug[:, p, 1, 4 * gr + j], p1[:, gr % 2, j],
                              start=False, stop=True)
                last.then_inc(s["pv"], 1)

            def transpose_o(i, qb):
                take_m()
                pe.wait_ge(s["o_ev"], i.times(2, 2))
                for gr in range(NG):
                    last = nc.tensor.transpose(M[:, gr * P:(gr + 1) * P], oT[:, gr, qb * P:(qb + 1) * P], ident[:, :])
                last.then_inc(s["otr_r"], 1)
                m_free[0] = [("on_d", i.times(2, qb + 1))]

            def transpose_on(i):
                take_m()
                pe.wait_ge(s["on_d"], i.times(2, 2))
                for qb in (0, 1):
                    last = nc.tensor.transpose(M[:, qb * P:(qb + 1) * P], on[:, qb].rearrange("p h v -> p (h v)"), ident[:, :])
                last.then_inc(s["onT_r"], 1)
                m_free[0] = [("onT_d", i.times(1, 1))]

            def project_o(i):
                take_m()
                for qb in (0, 1):
                    last = mm(M[:, qb * P:(qb + 1) * P], onT[:, qb * P:(qb + 1) * P], wat[:, 3], start=True, stop=True)
                last.then_inc(s["y_r"], 1)
                m_free[0] = [("y_d", i.times(1, 1))]

            def transpose_f(i):
                take_m()
                pe.wait_ge(s["f_d"], i.times(1, 1))
                for t in (0, 1):
                    last = nc.tensor.transpose(M[:, t * P:(t + 1) * P], fb[:, t], ident[:, :])
                last.then_inc(s["fT_r"], 1)
                m_free[0] = [("fT_d", i.times(1, 1))]

            def affinities(i):
                take_m()
                pe.wait_ge(s["fT_d"], i.times(1, 1))
                if i.k == 0:
                    pe.wait_ge(s["w_cent"], 16)
                for t in (0, 1):
                    last = mm(M[:, t * E:(t + 1) * E], fT[:, t], cent[:, :], start=True, stop=True)
                last.then_inc(s["aff_r"], 1)
                m_free[0] = [("aff_d", i.times(1, 1))]

            pe.wait_ge(s["consts"], 2)
            pe.wait_ge(s["w_attn"], 16)
            for n in (0, 1):
                transpose_x(Nth(n))
                project_qk(Nth(n))
                if n == 0:
                    project_v(Nth(n))
            transpose_x(Nth(2))
            pe.wait_ge(s["consts"], 6)
            for gr in range(NG):
                for u in range(3):
                    scores_by_query(Nth(0), gr, u)
                if gr == 1:
                    transpose_shift(Nth(0), 0)
                if gr == 2:
                    project_qk(Nth(2))

            def step(i):
                t, new, nxt, old, ln = at(i, 0), at(i, 3), at(i, 1), at(i, -1), at(i, -3)
                if UB < i.k < B - 2:
                    m_free[0] = [("hi_d", i.times(1, 3)), ("r1_d", i.times(1, 3))]
                elif B - 2 <= i.k < B + 2:
                    m_free[0] = [("y_d", i.times(1, -1))]
                for gr in range(NG):
                    if t:
                        scores_near(t, gr)
                    if nxt:
                        scores_by_query(nxt, gr, 0)
                    if gr == 0 and t:
                        transpose_shift(t, 1)
                    if gr == 1 and old:
                        transpose_o(old, 0)
                    if gr == 2 and nxt:
                        transpose_shift(nxt, 0)
                    if gr == 3 and old:
                        transpose_on(old)
                    if t:
                        scores_far(t, gr)
                    if nxt:
                        scores_by_query(nxt, gr, 1)
                    if gr == 0 and old:
                        weigh_values(old, 3)
                    if gr > 0 and t:
                        weigh_values(t, gr - 1)
                    if gr == 0 and ln:
                        transpose_f(ln)
                    if gr == 1 and old:
                        transpose_o(old, 1)
                    if gr == 2 and new:
                        transpose_x(new)
                    if gr == 3 and old:
                        project_o(old)
                    if nxt:
                        scores_by_query(nxt, gr, 2)
                    if gr == 1 and ln:
                        affinities(ln)
                    if gr == 2 and nxt:
                        project_v(nxt)
                    if gr == 3 and new:
                        project_qk(new)

            iterations(pe, step)

            pe.wait_ge(s["hot_d"], 1)
            hb = hotb[:, :, :].rearrange("p t e -> p (t e)")
            mm(M[:, 0:NT * E], before[:, :], hb, start=True, stop=True)
            mm(M[:, NT * E:2 * NT * E], onesb[:, :], hb, start=True, stop=True).then_inc(s["cnt_r"], 1)
            pe.wait_ge(s["rt"], 1)

            def enter(t):
                p = t.slot(2)
                pe.wait_ge(xs_in[t.slot(4)], t.turns(4, 16, 16))
                if t.follows(2):
                    pe.wait_ge(s["nT_d"], t.times(1, -1))
                nc.tensor.transpose((M, ST1[:, 0])[p][:, 0:P], xs[:, t.slot(4), 0:D], ident[:, :]).then_inc(s["xsT_r"], 1)

            def up(t):
                p = t.slot(2)
                pe.wait_ge(s["nT_d"], t.times(1, 1))
                for c in range(FC):
                    if t.follows(2) and c % 2 == 0:
                        pe.wait_ge(s["hd_d" if c else "ha_d"], t.times(1, -1))
                    last = mm(hidden(p, c), w1s[:, p, c * P:(c + 1) * P], nT[:, p], start=True, stop=True)
                    if c % 2:
                        last.then_inc(s["h_r"], 1)

            def down_(t):
                p = t.slot(2)
                if t.trip is None:
                    e = pe.value_load(eidx[0:1, t.k:t.k + 1], min_val=0, max_val=E - 1)
                else:
                    e = pe.value_load(eidx[0:1, bass.ds(t.times(1), 1)], min_val=0, max_val=E - 1)
                pe.wait_ge(s["ha_d"], t.times(1, 1))
                if t.follows(2):
                    pe.wait_ge(s["zo_d"], t.times(1, -1))
                for c in range(FC):
                    if c == FC // 2:
                        pe.wait_ge(s["hd_d"], t.times(1, 1))
                    last = mm(O[:, p, 0, 0:D], hs[:, p, c], w2_tab[:, bass.ds(e * (FC * D) + c * D, D)],
                              start=(c == 0), stop=(c == FC - 1))
                last.then_inc(s["z_r"], 1)

            def tile_step(t):
                if t.k + 2 < ST:
                    enter(t.plus(2))
                if 0 <= t.k + 1 < ST:
                    up(t.plus(1))
                if t.k >= 0:
                    down_(t)

            tiles(pe, tile_step)

        @block.vector
        def _(dve):
            v = nc.vector

            def x_stats(lo, hi, n):
                for t in range(lo, hi):
                    last = v.bn_stats(stx[:, t], x_all[:, t])
                last.then_inc(s["st_x"], 1)
                dve.wait_ge(s["st_x"], n)
                for t in range(lo, hi):
                    last = v.bn_aggr(mvx[:, t], stx[:, t])
                last.then_inc(s["agg_x"], 1)
                dve.wait_ge(s["agg_x"], n)
                v.tensor_scalar_add(vex[:, lo:hi], mvx[:, lo:hi, 1], EPS).then_inc(s["ve_x"], 1)

            v.memset(qaug[:, 0].bitcast(F32), 0.0).then_inc(s["qzero"], 1)
            dve.wait_ge(s["x_in"], 16)
            x_stats(0, 2 * RING, 1)
            v.memset(vaug[:, 0], 0.0).then_inc(s["vmem"], 1)
            dve.wait_ge(s["vmem"], 1)
            v.memset(vaug[:, 0, :, :, DH:DH + 1], 1.0).then_inc(s["vones"], 1)

            def normalise_x(b):
                p = b.slot(RING)
                if b.follows(RING):
                    dve.wait_ge(s["xnT_r"], b.times(1, 1 - RING))
                for t in (0, 1):
                    src = b.pick(x_all, 1, 2, t).rearrange("p o d -> p (o d)")
                    last = v.tensor_scalar(xn[:, p, t], src, b.pick(mvx, 1, 2, t)[:, :, 0], b.pick(rsx, 1, 2, t),
                                           ALU.subtract, ALU.mult)
                last.then_inc(s["xn_r"], 1)

            def residue(b):
                dve.wait_ge(s["hi_d"], b.times(1, 1))
                if b.follows(1):
                    dve.wait_ge(s["parts_d"], b.times(1))
                v.tensor_tensor(res1[:, :, :], M[:, :].rearrange("p (s t) -> p s t", s=2), part(b.slot(RING), 0),
                                ALU.subtract).then_inc(s["r1_d"], 1)

            def maxima(b, gr, u):
                p = b.slot(RING)
                n = 3 * gr + u
                dve.wait_ge(s["s_r"], b.times(12, n + 1))
                if u == 0:
                    dst, k = nmf[:, p, 4 * gr:4 * gr + 4, 0], 4
                else:
                    dst, k = nmf[:, p, 4 * gr + 2 * (u - 1):4 * gr + 2 * u, 1], 2
                v.tensor_reduce(dst, S[:, n % 2].rearrange("p (j n) -> p j n", j=k), op=ALU.max, axis=AX_X,
                                negate=True).then_inc(s["red"], 1)

            def shift_parts(b, half):
                p = b.slot(RING)
                src = nmf[:, p, 8 * half:8 * half + 8].rearrange("p h q -> p (h q)")
                dve.wait_ge(s["red"], b.times(12, 6 * half + 6))
                if b.follows(RING):
                    dve.wait_ge(s["shT_r"], b.times(2, half + 1 - 2 * RING))
                v.tensor_copy(nmp[:, p, half, 0], src).then_inc(s["nm_hi"], 1)
                dve.wait_ge(s["nm_hi"], b.times(2, half + 1))
                v.tensor_tensor(nmp[:, p, half, 1], src, nmp[:, p, half, 0], ALU.subtract).then_inc(s["nm_d"], 1)

            def divide(i, qb):
                mo = M[:, :].rearrange("p (h n) -> p h n", n=32)
                dve.wait_ge(s["otr_r"], i.times(2, qb + 1))
                v.reciprocal(rden[:, qb], mo[:, :, DH]).then_inc(s["rden_d"], 1)
                dve.wait_ge(s["rden_d"], i.times(2, qb + 1))
                if i.follows(1):
                    dve.wait_ge(s["onT_r"], i.times(1))
                v.tensor_tensor(on[:, qb], mo[:, :, 0:DH], rden[:, qb].unsqueeze(2).to_broadcast([P, NH, DH]),
                                ALU.mult).then_inc(s["on_d"], 1)

            def ln_src(b, n):
                if n == 0:
                    return lambda t: yb[:, b.slot(RING), t]
                if n == 1:
                    return lambda t: b.pick(x_all, 1, 2, t).rearrange("p o d -> p (o d)")
                return lambda t: fb[:, t]

            def ln_stats(b, n):
                if n == 0:
                    wait_fixed(dve, s["y_d"], b.times(1, 1))
                else:
                    wait_fixed(dve, s["x2_d" if n == 1 else "f_d"], b.times(1, 1))
                for t in (0, 1):
                    last = v.bn_stats(st_ln[:, n, t], ln_src(b, n)(t))
                last.then_inc(s["ln_st"], 1)

            def ln_aggregate(b, n):
                wait_fixed(dve, s["ln_st"], b.times(3, n + 1))
                for t in (0, 1):
                    last = v.bn_aggr(mv_ln[:, n, t], st_ln[:, n, t])
                last.then_inc(s["ln_ag"], 1)

            def ln_variance(b, n):
                dve.wait_ge(s["ln_ag"], b.times(3, n + 1))
                v.tensor_scalar_add(ve_ln[:, n], mv_ln[:, n, :, 1], EPS).then_inc(s["ln_ve"], 1)

            def ln_apply(b, n, dst, done):
                dve.wait_ge(s["ln_rs"], b.times(3, n + 1))
                for t in (0, 1):
                    last = v.tensor_scalar(dst(t), ln_src(b, n)(t), mv_ln[:, n, t, 0:1], rs_ln[:, n, t:t + 1],
                                           ALU.subtract, ALU.mult)
                last.then_inc(s[done], 1)

            def add_y(b):
                dve.wait_ge(s["yn_d"], b.times(1, 1))
                xb = b.pick(x_all, 2, 2)
                v.tensor_tensor(xb, xb, yn[:, :, :], ALU.add).then_inc(s["x2_d"], 1)

            dve.wait_ge(s["rs_x"], 1)
            normalise_x(Nth(0))
            normalise_x(Nth(1))
            v.memset(qaug[:, 1].bitcast(F32), 0.0).then_inc(s["qzero"], 1)
            residue(Nth(0))
            v.memset(qaug[:, 2].bitcast(F32), 0.0).then_inc(s["qzero"], 1)
            residue(Nth(1))
            normalise_x(Nth(2))
            dve.wait_ge(s["x_rest"], 16)
            x_stats(2 * RING, NT, 2)
            v.memset(vaug[:, 1], 0.0)
            v.memset(vaug[:, 2], 0.0).then_inc(s["vmem"], 1)
            dve.wait_ge(s["vmem"], 2)
            v.memset(vaug[:, 1, :, :, DH:DH + 1], 1.0).then_inc(s["vones"], 1)
            v.memset(vaug[:, 2, :, :, DH:DH + 1], 1.0).then_inc(s["vones"], 1)
            for gr in range(NG):
                for u in range(3):
                    maxima(Nth(0), gr, u)
                if gr % 2:
                    shift_parts(Nth(0), gr // 2)
                if gr == 2:
                    residue(Nth(2))
            dve.wait_ge(s["rs_x"], 2)

            def step(i):
                new, nxt, old, l2, l3 = at(i, 3), at(i, 1), at(i, -1), at(i, -2), at(i, -3)
                if new:
                    normalise_x(new)
                if nxt:
                    maxima(nxt, 0, 0)
                if l3:
                    if l3.k == 0:
                        dve.wait_ge(s["zero_w"], 16)
                    ln_apply(l3, 2, lambda t: l3.pick(pay, 1, 2, t).rearrange("p o d -> p (o d)")[:, 0:D], "pay_d")
                if l2:
                    ln_stats(l2, 0)
                if nxt:
                    maxima(nxt, 0, 1)
                if l2:
                    ln_aggregate(l2, 0)
                if nxt:
                    maxima(nxt, 0, 2)
                if l2:
                    ln_variance(l2, 0)
                if nxt:
                    maxima(nxt, 1, 0)
                if old:
                    divide(old, 0)
                if nxt:
                    maxima(nxt, 1, 1)
                if l2:
                    if l2.follows(1):
                        dve.wait_ge(s["x2_d"], l2.times(1))
                    ln_apply(l2, 0, lambda t: yn[:, t], "yn_d")
                if old:
                    divide(old, 1)
                if nxt:
                    maxima(nxt, 1, 2)
                    shift_parts(nxt, 0)
                if l2:
                    add_y(l2)
                if nxt:
                    maxima(nxt, 2, 0)
                if l2:
                    ln_stats(l2, 1)
                if nxt:
                    maxima(nxt, 2, 1)
                if l2:
                    ln_aggregate(l2, 1)
                if nxt:
                    maxima(nxt, 2, 2)
                if l2:
                    ln_variance(l2, 1)
                if nxt:
                    maxima(nxt, 3, 0)
                    maxima(nxt, 3, 1)
                if l2:
                    if l2.follows(1):
                        dve.wait_ge(s["fT_r"], l2.times(1))
                        dve.wait_ge(s["fc_d"], l2.times(1))
                    ln_apply(l2, 1, lambda t: fb[:, t], "f_d")
                    ln_stats(l2, 2)
                if nxt:
                    maxima(nxt, 3, 2)
                if l2:
                    ln_aggregate(l2, 2)
                if nxt:
                    shift_parts(nxt, 1)
                if l2:
                    ln_variance(l2, 2)
                if new:
                    residue(new)

            iterations(dve, step)

            chain = [0]

            def link(ins):
                chain[0] += 1
                ins.then_inc(s["tl"], 1)
                dve.wait_ge(s["tl"], chain[0])

            dve.wait_ge(s["aff_d"], B)
            dve.wait_ge(s["consts"], 9)
            link(v.tensor_reduce(amax[:, :], aff[:, :, :], op=ALU.max, axis=AX_X))
            by_t = amax[:, :].unsqueeze(2).to_broadcast([P, NT, E])
            link(v.tensor_tensor(hot[:, :, :], aff[:, :, :], by_t, ALU.is_equal))
            link(v.tensor_tensor(hot[:, :, :], hot[:, :, :], down[:, :].unsqueeze(1).to_broadcast([P, NT, E]), ALU.mult))
            link(v.tensor_reduce(key[:, :], hot[:, :, :], op=ALU.max, axis=AX_X))
            link(v.tensor_tensor(hot[:, :, :], hot[:, :, :], key[:, :].unsqueeze(2).to_broadcast([P, NT, E]), ALU.is_equal))
            v.tensor_copy(hotb[:, :, :], hot[:, :, :]).then_inc(s["hot_d"], 1)
            dve.wait_ge(s["cnt_r"], 1)
            v.tensor_copy(base[:, :, :], M[:, 0:NT * E].rearrange("p (t e) -> p t e", e=E))
            link(v.tensor_copy(cnt[:, 0], M[:, NT * E:2 * NT * E].rearrange("p (t e) -> p t e", e=E)))
            link(v.tensor_tensor(base[:, :, :], base[:, :, :], cnt[:, 0], ALU.subtract))
            cur, n = 0, 1
            while n < NT:
                v.tensor_copy(cnt[:, 1 - cur, 0:n], cnt[:, cur, 0:n])
                link(v.tensor_tensor(cnt[:, 1 - cur, n:NT], cnt[:, cur, n:NT], cnt[:, cur, 0:NT - n], ALU.add))
                cur, n = 1 - cur, 2 * n
            link(v.tensor_tensor(base[:, :, :], base[:, :, :], cnt[:, cur], ALU.add))
            link(v.tensor_tensor(above[:, :, :], cnt[:, cur, NT - 1].unsqueeze(2).to_broadcast([P, E, NT]),
                                 steps[:, :].unsqueeze(1).to_broadcast([P, E, NT]), ALU.is_gt))
            link(v.tensor_reduce(ntile[:, 0], above[:, :, :], op=ALU.add, axis=AX_X))
            tcur, n = 0, 1
            while n < E:
                v.tensor_copy(ntile[:, tcur + 1, 0:n], ntile[:, tcur, 0:n])
                link(v.tensor_tensor(ntile[:, tcur + 1, n:E], ntile[:, tcur, n:E], ntile[:, tcur, 0:E - n], ALU.add))
                tcur, n = tcur + 1, 2 * n
            link(v.tensor_tensor(tstart[:, :], ntile[:, tcur], ntile[:, 0], ALU.subtract))
            link(v.tensor_scalar(tstart[:, :], tstart[:, :], float(P), None, ALU.mult))
            link(v.tensor_tensor(base[:, :, :], base[:, :, :], tstart[:, :].unsqueeze(1).to_broadcast([P, NT, E]), ALU.add))
            link(v.tensor_tensor(base[:, :, :], base[:, :, :], hot[:, :, :], ALU.mult))
            link(v.tensor_reduce(posf[:, :], base[:, :, :], op=ALU.add, axis=AX_X))
            v.tensor_copy(pos[:, :], posf[:, :]).then_inc(s["pos_d"], 1)
            link(v.tensor_tensor(over[:, :, :], slots[:, :].unsqueeze(2).to_broadcast([P, ST, E]),
                                 ntile[:, tcur].unsqueeze(1).to_broadcast([P, ST, E]), ALU.is_ge))
            link(v.tensor_reduce(esel[:, :], over[:, :, :], op=ALU.add, axis=AX_X))
            link(v.tensor_scalar(esel[:, :], esel[:, :], float(E - 1), None, ALU.min))
            v.tensor_copy(eidx[:, :], esel[:, :]).then_inc(s["rt"], 1)
            dve.wait_ge(s["ex_d"], 1)
            link(v.tensor_scalar_add(eneg[:, :], eneg[:, :], 1.0))
            link(v.reciprocal(alpha[:, :], eneg[:, :]))
            dve.wait_ge(s["rt"], 1)
            dve.wait_ge(s["w_ffn"], 16 * (2 * E + 3))

            def expert(t):
                src = eidx[0:1, t.k:t.k + 1] if t.trip is None else eidx[0:1, bass.ds(t.times(1), 1)]
                return dve.value_load(src, min_val=0, max_val=E - 1)

            def weights(t):
                p = t.slot(2)
                e = expert(t)
                if t.follows(2):
                    dve.wait_ge(s["h_r"], t.times(2, -2))
                    dve.wait_ge(s["ha_d"], t.times(1, -1))
                    dve.wait_ge(s["hd_d"], t.times(1, -1))
                v.tensor_copy(w1s[:, p], w1_tab[:, bass.ds(e, 1), :].rearrange("p o n -> p (o n)")).then_inc(s["w1_d"], 1)

            def relu(t):
                p = t.slot(2)
                dve.wait_ge(s["w1_d"], t.times(1, 1))
                dve.wait_ge(s["h_r"], t.times(2, 2))
                if t.follows(2):
                    dve.wait_ge(s["z_r"], t.times(1, -1))
                for c in range(FC // 2, FC):
                    last = v.tensor_scalar(hs[:, p, c], hidden(p, c), w1s[:, p, F + 2 + c:F + 3 + c], 0.0, ALU.add, ALU.max)
                last.then_inc(s["hd_d"], 1)

            def leave(t):
                q = t.slot(4)
                e = expert(t)
                dve.wait_ge(xs_in[q], t.turns(4, 16, 16))
                if t.follows(4):
                    dve.wait_ge(z_sc[q], t.turns(4, 16))
                v.tensor_copy(ids[:, q:q + 1], xs[:, q, D:ROW].bitcast(I32)).then_inc(s["id_d"], 1)
                dve.wait_ge(s["z_r"], t.times(1, 1))
                v.tensor_tensor(zo[:, q], O[:, t.slot(2), 0, 0:D], b2_tab[:, bass.ds(e * D, D)], ALU.add).then_inc(s["zo_d"], 1)

            def tile_step(t):
                if t.k + 2 < ST:
                    weights(t.plus(2))
                if 0 <= t.k + 1 < ST:
                    relu(t.plus(1))
                if t.k >= 0:
                    leave(t)

            tiles(dve, tile_step)

            def z_bias(c):
                q = slice(4 * c, 4 * c + 4)
                dve.wait_ge(s["rs_z"], c + 1)
                v.scalar_tensor_tensor(out=nbz[:, q], in0=mvz[:, q, 0], scalar=-1.0, in1=rsz[:, q],
                                       op0=ALU.mult, op1=ALU.mult).then_inc(s["nb_z"], 1)

            for c in range(NT // 4):
                q = slice(4 * c, 4 * c + 4)
                dve.wait_ge(z_in[c], 16)
                for t in range(4 * c, 4 * c + 4):
                    last = v.scalar_tensor_tensor(out=z_all[:, t], in0=z_all[:, t], scalar=alpha[:, t:t + 1], in1=f_all[:, t],
                                                  op0=ALU.mult, op1=ALU.add)
                last.then_inc(s["zf_d"], 1)
                dve.wait_ge(s["zf_d"], c + 1)
                for t in range(4 * c, 4 * c + 4):
                    last = v.bn_stats(stz[:, t], z_all[:, t])
                last.then_inc(s["st_z"], 1)
                dve.wait_ge(s["st_z"], c + 1)
                for t in range(4 * c, 4 * c + 4):
                    last = v.bn_aggr(mvz[:, t], stz[:, t])
                last.then_inc(s["agg_z"], 1)
                dve.wait_ge(s["agg_z"], c + 1)
                v.tensor_scalar_add(vez[:, q], mvz[:, q, 1], EPS).then_inc(s["ve_z"], 1)
                if c >= 1:
                    z_bias(c - 1)
            z_bias(NT // 4 - 1)


def kernel(L0_attn_x, L0_attn_WQ, L0_attn_WK, L0_attn_WV, L0_attn_WO, L0_ffn_centroids, L0_ffn_ln_g, L0_ffn_ln_b,
           L0_ffn_w1, L0_ffn_b1, L0_ffn_w2, L0_ffn_b2):
    import concourse.bacc as bacc
    from concourse.bass_utils import run_bass_kernel_spmd

    nh, dh, d = L0_attn_WQ.shape
    e, f, _ = L0_ffn_w1.shape
    attn_w = np.stack([np.asarray(w).transpose(2, 1, 0).reshape(d, nh * dh) for w in (L0_attn_WQ, L0_attn_WK)]
                      + [np.asarray(L0_attn_WV).reshape(nh * dh, d).T]
                      + [np.asarray(L0_attn_WO).transpose(0, 2, 1).reshape(nh * dh, d)])
    w1t = np.asarray(L0_ffn_w1).transpose(0, 2, 1)
    w2t = np.asarray(L0_ffn_w2).reshape(e, d, f // 128, 128).transpose(3, 0, 2, 1).reshape(128, -1)
    ln_cols = np.stack([np.asarray(L0_ffn_ln_g), np.asarray(L0_ffn_ln_b)], axis=-1).transpose(1, 0, 2)
    b1_cols = np.asarray(L0_ffn_b1).reshape(e, f // 128, 128).transpose(2, 0, 1)
    arrays = {"x": L0_attn_x, "attn_w": attn_w, "w1t": w1t, "w2t": w2t, "ln_cols": ln_cols, "b1_cols": b1_cols,
              "b2": L0_ffn_b2, "cent_t": np.asarray(L0_ffn_centroids).T}
    nc = bacc.Bacc("TRN2", target_bir_lowering=False, num_devices=1)
    ins, args = {}, {}
    for name, value in arrays.items():
        value = np.ascontiguousarray(value)
        ins[f"in_{name}"] = value
        args[name] = nc.dram_tensor(f"in_{name}", value.shape, mybir.dt.from_np(value.dtype), kind="ExternalInput").ap()
    out = nc.dram_tensor("out_x", tuple(L0_attn_x.shape), F32, kind="ExternalOutput").ap()
    sandwich_kernel(nc, out=out, **args)
    return run_bass_kernel_spmd(nc, [ins], core_ids=[0]).results[0]["out_x"]
```

```python
from contextlib import ExitStack

import numpy as np

import concourse.bass as bass
from concourse import mybir

ALU = mybir.AluOpType
ACT = mybir.ActivationFunctionType
AX_X = mybir.AxisListType.X
F32 = mybir.dt.float32
BF16 = mybir.dt.bfloat16
I32 = mybir.dt.int32
U32 = mybir.dt.uint32

P = 128
EPS = 1e-5
NEG = -1e30


class Nth:

    def __init__(self, k, trip=None, unroll=1):
        self.k, self.trip, self.unroll = k, trip, unroll

    def plus(self, n):
        return Nth(self.k + n, self.trip, self.unroll)

    def times(self, a, b=0):
        return a * self.k + b if self.trip is None else self.trip * (self.unroll * a) + (a * self.k + b)

    def turns(self, ring, a, b=0):
        here = a * (self.k // ring) + b
        return here if self.trip is None else self.trip * (self.unroll // ring * a) + here

    def slot(self, ring):
        assert self.trip is None or self.unroll % ring == 0
        return self.k % ring

    def follows(self, n):
        return self.k >= n

    def pick(self, table, width=1, step=1, b=0):
        at = self.times(step, b)
        if self.trip is None:
            return table[:, at:at + width]
        return table[:, bass.ds(at, width)]


def sandwich_kernel(nc, x, attn_w, w1t, w2t, ln_cols, b1_cols, b2, cent_t, out):
    B, SEQ, D = x.shape
    NH = 16
    DH = D // NH
    E, _, F = w1t.shape
    NT = B * SEQ // P
    FC = F // P
    NG = NH // 4
    SCALE = float(DH) ** -0.5
    ST = NT + E - 1
    TOK, ALPHA, MEAN, VAR, RSTD, SHFT = range(2 * D, 2 * D + 6)
    ROW = 2 * D + 6
    CAP = (NT + 1) * P
    SP1 = F + 2 + FC
    assert D == P and SEQ == 2 * P and B % 2 == 0

    RING = 3
    UB, UT = 3, 8
    NPAIR = 6
    SHIFT = P - 2

    xs_dram = nc.dram_tensor("xs_rows", (E * CAP + P, ROW), F32, kind="Internal").ap()
    qk_dram = nc.dram_tensor("qk_parts", (RING, 2, 3, DH, NH, SEQ), BF16, kind="Internal").ap()
    sh_dram = nc.dram_tensor("shift_rows", (RING, 2, 2, 8 * SEQ), BF16, kind="Internal").ap()

    with ExitStack() as ctx:
        def sb(name, shape, dt=F32):
            return ctx.enter_context(nc.sbuf_tensor(name, shape, dt))

        def ps(name, shape, dt=F32):
            return ctx.enter_context(nc.psum_tensor(name, shape, dt))

        def sem(name):
            return ctx.enter_context(nc.semaphore(name))

        wat = sb("wat", [P, 4, D])
        w1_tab = sb("w1_tab", [P, E, SP1])
        w2_tab = sb("w2_tab", [P, E * FC * D])
        b2_tab = sb("b2_tab", [P, E * D])
        cent = sb("cent", [P, E])
        ident = sb("ident", [P, P])
        identb = sb("identb", [P, P], BF16)
        causal = sb("causal", [P, 4, P], BF16)
        before = sb("before", [P, P])
        ones = sb("ones", [P, P])
        mhalf = sb("mhalf", [P, NT])
        x_all = sb("x_all", [P, NT, D])
        pay = sb("pay", [P, RING, 2, ROW])
        fill = sb("fill", [P, ROW])
        fill_at = sb("fill_at", [P, 1], I32)
        mvx = sb("mvx", [P, NT, 2])
        vex = sb("vex", [P, NT])
        rsx = sb("rsx", [P, NT])
        stx = sb("stx", [P, NT, 6])
        xn = sb("xn", [P, RING, 2, D])
        xnT = sb("xnT", [P, RING, SEQ])
        qkp = sb("qkp", [P, RING, 6, SEQ], BF16)
        res1 = sb("res1", [P, 2, SEQ])
        aug = sb("aug", [P, 2 * RING * NH * SEQ], BF16)
        augv = aug[:, :].rearrange("p (s r h t) -> p s r h t", s=2, r=RING, h=NH)
        qaug, kaug = augv[:, 0], augv[:, 1]
        nmf = sb("nmf", [P, RING, NH, 2])
        nmp = sb("nmp", [P, RING, 2, 2, 16], BF16)
        nmT = sb("nmT", [32, RING, 2, P], BF16)
        vaug = sb("vaug", [P, RING, 2, NH, 32])
        p0 = sb("p0", [P, 2, 4, SEQ])
        p1 = sb("p1", [P, 2, 4, P])
        oT = sb("oT", [P, 4, SEQ])
        rden = sb("rden", [P, 2, NH])
        on = sb("on", [P, 2, NH, DH])
        onT = sb("onT", [P, SEQ])
        yb = sb("yb", [P, RING, 2, D])
        yn = sb("yn", [P, 2, D])
        st_ln = sb("st_ln", [P, 3, 2, 6])
        mv_ln = sb("mv_ln", [P, 3, 2, 2])
        ve_ln = sb("ve_ln", [P, 3, 2])
        rs_ln = sb("rs_ln", [P, 3, 2])
        fT = sb("fT", [P, 2, P])
        aff = sb("aff", [P, NT, E])
        amax = sb("amax", [P, NT])
        eneg = sb("eneg", [P, NT])
        down = sb("down", [P, E])
        steps = sb("steps", [P, NT])
        slots = sb("slots", [P, ST])
        starts = sb("starts", [P, E])
        hotk = sb("hotk", [P, NT, E])
        key = sb("key", [P, NT])
        hot = sb("hot", [P, NT, E])
        run = sb("run", [P, NT + 1, E])
        rank = sb("rank", [P, NT, E])
        posw = sb("posw", [P, NT, E])
        posf = sb("posf", [P, NT])
        pos = sb("pos", [P, RING, 2], I32)
        tokid = sb("tokid", [P, NT], I32)
        cnt = sb("cnt", [P, E])
        ends = sb("ends", [P, E], I32)
        above = sb("above", [P, E, NT])
        ntile = sb("ntile", [P, 4, E])
        over = sb("over", [P, 2, ST, E])
        skip = sb("skip", [P, E])
        esel = sb("esel", [P, ST])
        rowf = sb("rowf", [P, 2, ST])
        eidx = sb("eidx", [P, ST], I32)
        rows_at = sb("rows_at", [P, ST], I32)
        def carve(table, *shapes):
            flat = table[:].rearrange("p a b c d -> p (a b c d)" if len(table.shape) == 5 else
                                      "p a b c -> p (a b c)" if len(table.shape) == 4 else "p a b -> p (a b)")
            at, views = 0, []
            for shape in shapes:
                n = int(np.prod(shape))
                view = flat[:, at:at + n]
                if len(shape) == 2:
                    view = view.rearrange("p (a b) -> p a b", b=shape[1])
                if len(shape) == 3:
                    view = view.rearrange("p (a b c) -> p a b c", b=shape[1], c=shape[2])
                views.append(view)
                at += n
            return views

        xs, w1s = carve(x_all, (UT, ROW), (2, SP1))
        nh, nT, hs, zb, zf, zn, zo = carve(vaug, (2, D), (2, P), (2, FC, P), (2, D), (2, D), (2, D), (2, D))
        stz = sb("stz", [P, 2, 6])
        mvz = sb("mvz", [P, 2, 2])
        vez = sb("vez", [P, 2])
        rsz = sb("rsz", [P, 2])
        ids = sb("ids", [P, 2], I32)
        nbz = sb("nbz", [P, 2])

        S = ps("S", [P, 2, 512])
        ST0 = ps("ST0", [P, 4, SEQ])
        ST1 = ps("ST1", [P, 4, P])
        O = ps("O", [P, 2, 2, SEQ])
        M = ps("M", [P, 512])

        names = ("w_attn w_cent w_ffn x_in x_next x_rest qzero kone ids_r consts pmem vmem vones "
                 "st_x agg_x ve_x rs_x xn_r xnT_r xnT_d qk_r hi_d r1_d mid_d parts_d "
                 "v_r v_d s_r red nm_hi nm_d shT_r sh_d st0_r st1_r exp0 exp1 sel0 sel1 pv o_ev "
                 "otr_r rden_d on_d onT_r onT_d y_r y_d "
                 "ln_st ln_ag ln_ve ln_rs yn_d x2_d f_d fT_r fT_d ar_r ar_d id_in "
                 "ln_sh chosen ex_d al_p al_d run_d pw_d pf_d pos_d total_r tl ends_d rt pads "
                 "w1_d nh_d xsT_r nT_d h_r ha_d hd_d z_r zb_d zf_d st_z agg_z ve_z rs_z nb_z zn_d zo_d").split()
        s = {n: sem(n) for n in names}
        qk_w = [sem(f"qk_w{p}") for p in range(RING)]
        aug_in = [sem(f"aug_in{p}") for p in range(RING)]
        sh_w = [sem(f"sh_w{h}") for h in (0, 1)]
        sh_in = [sem(f"sh_in{h}") for h in (0, 1)]
        FIRST_SCAT = (UB + 1 - 2) % RING
        scat = [sem(f"scat{p}") for p in range(RING)]
        xs_in = [sem(f"xs_in{p}") for p in range(UT)]
        out_s = [sem(f"out_s{p}") for p in (0, 1)]

        STATS = [(0, 2), (2, 2 * RING), (2 * RING, 4 * RING), (4 * RING, NT // 2 + 2 * RING), (NT // 2 + 2 * RING, NT)]

        block = ctx.enter_context(nc.Block())
        LAST = B - 1

        def part(p, c):
            return qkp[:, p, c:6 - c:5 - 2 * c, :]

        NA = FC // 2

        def hidden(p, c):
            if c < NA:
                return S[:, p, c * P:(c + 1) * P]
            return ST0[:, 2 * p:2 * p + 2].rearrange("p a n -> p (a n)")[:, (c - NA) * P:(c - NA + 1) * P]

        def wait_fixed(eng, name, value):
            if not isinstance(value, int):
                value = eng.compute_val(value)
            eng.wait_ge(s["consts"], 1)
            eng.wait_ge(name, value)

        def iterations(eng, step):
            first = UB + 1
            trips = (B - 3 - first) // UB
            for i in range(first):
                step(Nth(i))
            with eng.Fori(0, trips) as trip:
                for k in range(UB):
                    step(Nth(first + k, trip, UB))
            for i in range(first + trips * UB, B + 4):
                step(Nth(i))

        def tiles(eng, step):
            first = 5
            trips = (ST - 3 - first) // UT
            for k in range(-3, first):
                step(Nth(k))
            with eng.Fori(0, trips) as trip:
                for k in range(UT):
                    step(Nth(first + k, trip, UT))
            for k in range(first + trips * UT, ST + 3):
                step(Nth(k))

        def tile(t, stage):
            n = t.plus(stage)
            return n if t.trip is not None or 0 <= n.k < ST else None

        def expert(eng, t):
            return eng.value_load(t.pick(eidx)[0:1], min_val=0, max_val=E - 1)

        def at(i, stage):
            b = i.plus(stage)
            return b if 0 <= b.k <= LAST else None

        def pad(eng, experts):
            for e in experts:
                end = eng.value_load(ends[0:1, e:e + 1], min_val=e * CAP, max_val=(e + 1) * CAP - P)
                eng.dma_start(xs_dram[bass.ds(end, P), :], fill[:, :]).then_inc(s["pads"], 16)

        @block.sync
        def _(sp):
            xv = x.rearrange("b (t p) d -> p (b t) d", p=P)
            sp.dma_start(x_all[:, 0:2, :], xv[:, 0:2, :]).then_inc(s["x_in"], 16)
            sp.dma_start(wat[:, :, :], attn_w.rearrange("k p n -> p k n")).then_inc(s["w_attn"], 16)
            sp.dma_start(x_all[:, 2:2 * RING, :], xv[:, 2:2 * RING, :]).then_inc(s["x_next"], 16)
            sp.dma_start(x_all[:, 2 * RING:NT, :], xv[:, 2 * RING:NT, :]).then_inc(s["x_rest"], 16)

            def parts_out(b):
                p = b.slot(RING)
                wait_fixed(sp, s["parts_d"], b.times(1, 1))
                if b.follows(RING):
                    wait_fixed(sp, aug_in[p], b.turns(RING, 96))
                sp.dma_start(qk_dram[p].rearrange("s c d h t -> (d h) (s c) t"), qkp[:, p]).then_inc(qk_w[p], 16)

            def parts_in(b):
                p = b.slot(RING)
                wait_fixed(sp, qk_w[p], b.turns(RING, 16, 16))
                if b.follows(RING):
                    wait_fixed(sp, s["st1_r"], b.times(NG, -NG * (RING - 1)))
                row = 0
                for n in (3, 2, 1):
                    rows = n * DH
                    sp.dma_start(qaug[row:row + rows, p], qk_dram[p, 0, 0:n].rearrange("c d h t -> (c d) h t"))\
                        .then_inc(aug_in[p], 16)
                    sp.dma_start(kaug[row:row + rows, p], qk_dram[p, 1, 3 - n:3].rearrange("c d h t -> (c d) h t"))\
                        .then_inc(aug_in[p], 16)
                    row += rows

            def shift(b, half):
                p = b.slot(RING)
                wait_fixed(sp, sh_w[half], b.times(16, 16))
                if b.follows(RING):
                    wait_fixed(sp, s["st1_r"], b.times(NG, -NG * (RING - 1)))
                sp.dma_start(qaug[SHIFT:P, p, 8 * half:8 * half + 8],
                             sh_dram[p, half].rearrange("c (h t) -> c h t", t=SEQ)).then_inc(sh_in[half], 16)

            parts_out(Nth(0))
            sp.wait_ge(s["qzero"], 1)
            sp.wait_ge(s["kone"], 1)
            parts_in(Nth(0))
            parts_out(Nth(1))
            sp.wait_ge(s["qzero"], 3)
            sp.wait_ge(s["kone"], 3)
            parts_in(Nth(1))
            shift(Nth(0), 0)

            def step(i):
                if b := at(i, 0):
                    shift(b, 1)
                if b := at(i, 2):
                    parts_out(b)
                if b := at(i, 2):
                    parts_in(b)
                if b := at(i, 1):
                    shift(b, 0)
                if i.trip is None and i.k <= B:
                    e = i.k if i.k <= UB else i.k - (B + 1 - E)
                    sp.dma_start(w1_tab[:, e, 0:F], w1t[e]).then_inc(s["w_ffn"], 16)
                    sp.dma_start(w2_tab[:, e * FC * D:(e + 1) * FC * D], w2t[:, e * FC * D:(e + 1) * FC * D])\
                        .then_inc(s["w_ffn"], 16)
                if i.k == 0:
                    sp.dma_start(cent[:, :], cent_t).then_inc(s["w_cent"], 16)
                    sp.dma_start(w1_tab[:, :, F:F + 2], ln_cols).then_inc(s["w_ffn"], 16)
                    sp.dma_start(w1_tab[:, :, F + 2:SP1], b1_cols).then_inc(s["w_ffn"], 16)
                    sp.dma_start(b2_tab[:, :], b2.rearrange("(o e) d -> o (e d)", o=1).to_broadcast([P, E * D]))\
                        .then_inc(s["w_ffn"], 16)
            iterations(sp, step)

            sp.wait_ge(s["ends_d"], 1)
            pad(sp, range(0, E, 2))

            sp.wait_ge(s["rt"], 1)
            for p in range(RING):
                sp.wait_ge(scat[p], 32 * len(range(p, B, RING)) + 16 * (p == FIRST_SCAT))
            sp.wait_ge(s["pads"], 16 * E)

            def rows_in(t):
                q = t.slot(UT)
                row = sp.value_load(t.pick(rows_at)[0:1], min_val=0, max_val=E * CAP)
                if t.follows(UT):
                    wait_fixed(sp, s["zo_d"], t.times(1, 1 - UT))
                sp.dma_start(xs[:, q], xs_dram[bass.ds(row, P), :]).then_inc(xs_in[q], 16)

            for t in range(UT):
                rows_in(Nth(t))
            trips = ST // UT - 1
            with sp.Fori(0, trips) as trip:
                for k in range(UT):
                    rows_in(Nth(UT + k, trip, UT))
            for t in range(UT * (trips + 1), ST):
                rows_in(Nth(t))
            for p in (0, 1):
                sp.wait_ge(out_s[p], 16 * len(range(p, ST, 2)))

        @block.gpsimd
        def _(pool):
            g = nc.gpsimd
            two_ones = float(np.array([0x3F803F80], np.uint32).view(np.float32)[0])
            g.memset(ident[:, :], 0.0).then_inc(s["pmem"], 1)
            g.memset(mhalf[:, :], -0.5).then_inc(s["consts"], 1)
            pool.wait_ge(s["pmem"], 1)
            g.affine_select(out=ident[:, :], in_=ident[:, :], compare_op=ALU.not_equal, fill=1.0, base=0,
                            pattern=[[-1, P]], channel_multiplier=1).then_inc(s["consts"], 1)

            def power_x(n):
                lo, hi = STATS[n]
                pool.wait_ge(s["ve_x"], n + 1)
                g.tensor_tensor(rsx[:, lo:hi], vex[:, lo:hi], mhalf[:, lo:hi], op=ALU.pow).then_inc(s["rs_x"], 1)

            pool.wait_ge(s["consts"], 2)
            power_x(0)
            power_x(1)
            g.memset(kaug[:, 0].bitcast(F32), two_ones).then_inc(s["kone"], 1)

            def low(b):
                p = b.slot(RING)
                pool.wait_ge(s["mid_d"], b.times(1, 1))
                if b.follows(RING):
                    pool.wait_ge(qk_w[p], b.turns(RING, 16))
                g.tensor_tensor(part(p, 2), res1[:, :, :], part(p, 1), op=ALU.subtract).then_inc(s["parts_d"], 1)

            def select(i, gr):
                v = p0[:, gr % 2, :, 0:P]
                wait_fixed(pool, s["exp0"], i.times(NG, gr + 1))
                g.affine_select(out=v, in_=v, compare_op=ALU.is_ge, fill=0.0, base=0,
                                pattern=[[0, 4], [1, P]], channel_multiplier=-1).then_inc(s["sel0"], 1)
                wait_fixed(pool, s["exp1"], i.times(NG, gr + 1))
                v = p1[:, gr % 2]
                g.affine_select(out=v, in_=v, compare_op=ALU.is_ge, fill=0.0, base=0,
                                pattern=[[0, 4], [1, P]], channel_multiplier=-1).then_inc(s["sel1"], 1)

            def power(b, n):
                pool.wait_ge(s["ln_ve"], b.times(3, n + 1))
                dst = rs_ln[:, n] if n < 2 else pay[:, b.slot(RING), :, RSTD]
                g.tensor_tensor(dst, ve_ln[:, n], mhalf[:, 0:2], op=ALU.pow).then_inc(s["ln_rs"], 1)

            def number(b):
                wait_fixed(pool, s["x2_d"], b.times(1, 1))
                g.tensor_copy(pay[:, b.slot(RING), :, TOK].bitcast(I32), b.pick(tokid, 2, 2)).then_inc(s["id_in"], 1)

            def scatter(b, t):
                p = b.slot(RING)
                if t == 0:
                    wait_fixed(pool, s["ln_sh"], b.times(1, 1))
                    wait_fixed(pool, s["id_in"], b.times(1, 1))
                    wait_fixed(pool, s["al_d"], b.times(1, 1))
                    wait_fixed(pool, s["pos_d"], b.times(1, 1))
                g.indirect_dma_start(out=xs_dram, out_offset=bass.IndirectOffsetOnAxis(ap=pos[:, p, t:t + 1].bitcast(U32), axis=0),
                                     in_=pay[:, p, t, :], in_offset=None).then_inc(scat[p], 16)

            low(Nth(0))
            g.memset(causal[:, :, :], 0.0).then_inc(s["pmem"], 1)
            g.memset(before[:, :], 1.0).then_inc(s["pmem"], 1)
            g.memset(ones[:, :], 1.0).then_inc(s["consts"], 1)
            g.tensor_copy(identb[:, :], ident[:, :]).then_inc(s["consts"], 1)
            pool.wait_ge(s["pmem"], 3)
            g.affine_select(out=causal[:, :, :], in_=causal[:, :, :], compare_op=ALU.is_ge, fill=NEG, base=0,
                            pattern=[[0, 4], [-1, P]], channel_multiplier=1).then_inc(s["consts"], 1)
            g.affine_select(out=before[:, :], in_=before[:, :], compare_op=ALU.is_gt, fill=0.0, base=0,
                            pattern=[[1, P]], channel_multiplier=-1).then_inc(s["consts"], 1)
            g.memset(kaug[:, 1].bitcast(F32), two_ones).then_inc(s["kone"], 1)
            g.memset(kaug[:, 2].bitcast(F32), two_ones).then_inc(s["kone"], 1)
            low(Nth(1))
            power_x(2)
            g.iota(tokid[:, :], [[P, NT]], base=0, channel_multiplier=1).then_inc(s["ids_r"], 1)
            g.memset(fill[:, :], 0.0).then_inc(s["ids_r"], 1)
            g.iota(fill_at[:, :], [[0, 1]], base=E * CAP, channel_multiplier=1).then_inc(s["ids_r"], 1)
            for table, by, base in ((down, -1, E), (steps, P, 0), (slots, 1, 0), (starts, CAP, 0), (run[:, 0], CAP // P, 0)):
                g.iota(table[:, :], [[by, table.shape[-1]]], base=base, channel_multiplier=0,
                       allow_small_or_imprecise_dtypes=True).then_inc(s["consts"], 1)
            pool.wait_ge(s["ids_r"], 3)
            g.iota(fill[:, TOK:TOK + 1].bitcast(I32), [[0, 1]], base=NT * P, channel_multiplier=1).then_inc(s["ids_r"], 1)
            pool.wait_ge(s["ids_r"], 4)
            g.indirect_dma_start(out=xs_dram, out_offset=bass.IndirectOffsetOnAxis(ap=fill_at[:, 0:1].bitcast(U32), axis=0),
                                 in_=fill[:, :], in_offset=None).then_inc(scat[FIRST_SCAT], 16)
            low(Nth(2))

            def step(i):
                t, ln, last = at(i, 0), at(i, -2), at(i, -4)
                if t:
                    select(t, 0)
                    select(t, 1)
                if ln:
                    power(ln, 0)
                if t:
                    select(t, 2)
                if ln:
                    power(ln, 1)
                if t:
                    select(t, 3)
                if last:
                    scatter(last, 0)
                if ln:
                    power(ln, 2)
                if last:
                    scatter(last, 1)
                if ln:
                    number(ln)
                if i.k < 2:
                    power_x(i.k + 3)
                if b := at(i, 3):
                    low(b)

            iterations(pool, step)

            def leave(t):
                p = t.slot(2)
                wait_fixed(pool, s["zo_d"], t.times(1, 1))
                g.indirect_dma_start(out=out.rearrange("b t d -> (b t) d"),
                                     out_offset=bass.IndirectOffsetOnAxis(ap=ids[:, p:p + 1].bitcast(U32), axis=0),
                                     in_=zo[:, p, :], in_offset=None, bounds_check=NT * P - 1, oob_is_err=False)\
                    .then_inc(out_s[p], 16)

            def power_z(t):
                p = t.slot(2)
                wait_fixed(pool, s["ve_z"], t.times(1, 1))
                g.tensor_tensor(rsz[:, p:p + 1], vez[:, p:p + 1], mhalf[:, 0:1], op=ALU.pow).then_inc(s["rs_z"], 1)

            def tile_step(t):
                if n := tile(t, -3):
                    leave(n)
                if n := tile(t, -1):
                    power_z(n)

            tiles(pool, tile_step)

        @block.scalar
        def _(act):
            a = nc.scalar

            def xnT_out(b):
                p = b.slot(RING)
                act.wait_ge(s["xnT_r"], b.times(1, 1))
                if b.follows(RING):
                    act.wait_ge(s["v_r"], b.times(1, 1 - RING))
                a.activation(xnT[:, p], M[:, 0:SEQ], ACT.Copy).then_inc(s["xnT_d"], 1)

            def high(b):
                p = b.slot(RING)
                act.wait_ge(s["qk_r"], b.times(1, 1))
                if b.follows(RING):
                    act.wait_ge(qk_w[p], b.turns(RING, 16))
                a.activation(part(p, 0), M[:, :].rearrange("p (s t) -> p s t", s=2), ACT.Copy).then_inc(s["hi_d"], 1)

            def middle(b):
                p = b.slot(RING)
                act.wait_ge(s["r1_d"], b.times(1, 1))
                a.activation(part(p, 1), res1[:, :, :], ACT.Copy).then_inc(s["mid_d"], 1)

            def shift_out(b, half):
                act.wait_ge(s["shT_r"], b.times(2, half + 1))
                if b.follows(RING):
                    act.wait_ge(sh_w[half], b.times(16, 16 * (1 - RING)))
                p = b.slot(RING)
                a.activation(nmT[:, p, half], M[:, 0:P // 2].bitcast(BF16)[0:32, 0:P], ACT.Copy).then_inc(s["sh_d"], 1)
                wait_fixed(act, s["sh_d"], b.times(2, half + 1))
                if b.follows(RING):
                    wait_fixed(act, sh_in[half], b.times(16, -16 * (RING - 1)))
                act.dma_start(sh_dram[p, half].rearrange("c (r t) -> (c r) t", t=P), nmT[:, p, half])\
                    .then_inc(sh_w[half], 16)

            def v_out(b):
                p = b.slot(RING)
                act.wait_ge(s["v_r"], b.times(1, 1))
                if b.follows(RING):
                    act.wait_ge(s["pv"], b.times(NG, NG * (1 - RING)))
                else:
                    act.wait_ge(s["vones"], p + 1)
                a.activation(vaug[:, p, :, :, 0:DH], M[:, 0:SEQ].rearrange("p (t h d) -> p t h d", t=2, d=DH),
                             ACT.Copy).then_inc(s["v_d"], 1)

            def exp_near(i, gr):
                act.wait_ge(s["st0_r"], i.times(NG, gr + 1))
                if i.k > 0 or gr >= 2:
                    act.wait_ge(s["pv"], i.times(NG, gr - 1))
                a.activation(p0[:, gr % 2], ST0[:, :, :], ACT.Exp, scale=SCALE).then_inc(s["exp0"], 1)

            def exp_far(i, gr):
                act.wait_ge(s["st1_r"], i.times(NG, gr + 1))
                a.activation(p1[:, gr % 2], ST1[:, :, :], ACT.Exp, scale=SCALE).then_inc(s["exp1"], 1)

            def o_out(i, half):
                act.wait_ge(s["pv"], i.times(NG, 2 * half + 2))
                if i.follows(1):
                    act.wait_ge(s["otr_r"], i.times(2))
                a.activation(oT[:, 2 * half:2 * half + 2], O[:, half], ACT.Copy).then_inc(s["o_ev"], 1)

            def onT_out(i):
                act.wait_ge(s["onT_r"], i.times(1, 1))
                if i.follows(1):
                    act.wait_ge(s["y_r"], i.times(1))
                a.activation(onT[:, :], M[:, 0:SEQ], ACT.Copy).then_inc(s["onT_d"], 1)

            def y_out(i):
                act.wait_ge(s["y_r"], i.times(1, 1))
                if i.follows(RING):
                    act.wait_ge(s["yn_d"], i.times(1, 1 - RING))
                a.activation(yb[:, i.slot(RING)], M[:, 0:SEQ].rearrange("p (t d) -> p t d", t=2), ACT.Copy).then_inc(s["y_d"], 1)

            def fT_out(i):
                act.wait_ge(s["fT_r"], i.times(1, 1))
                if i.follows(1):
                    act.wait_ge(s["ar_r"], i.times(1))
                a.activation(fT[:, :, :], M[:, 0:SEQ].rearrange("p (t n) -> p t n", t=2), ACT.Copy).then_inc(s["fT_d"], 1)

            def affinities_and_ranks_out(n, ln, last):
                act.wait_ge(s["ar_r"], n.times(1, 1))
                if ln:
                    ins = a.activation(ln.pick(aff, 2, 2), M[:, 0:2 * E].rearrange("p (t e) -> p t e", e=E), ACT.Copy)
                if last:
                    ins = a.activation(last.pick(rank, 2, 2), M[:, 2 * E:4 * E].rearrange("p (t e) -> p t e", e=E), ACT.Copy)
                ins.then_inc(s["ar_d"], 1)

            def exp_negative(i):
                act.wait_ge(s["chosen"], i.times(4, 1))
                a.activation(i.pick(eneg, 2, 2), i.pick(amax, 2, 2), ACT.Exp, scale=-1.0).then_inc(s["ex_d"], 1)

            for n in (0, 1):
                xnT_out(Nth(n))
                high(Nth(n))
                middle(Nth(n))
                if n == 0:
                    v_out(Nth(n))
            xnT_out(Nth(2))
            shift_out(Nth(0), 0)
            high(Nth(2))
            middle(Nth(2))

            def step(i):
                t, new, nxt, old, l2, ln, last = (at(i, n) for n in (0, 3, 1, -1, -2, -3, -4))
                if t:
                    exp_near(t, 0)
                if l2:
                    y_out(l2)
                if t:
                    exp_far(t, 0)
                    shift_out(t, 1)
                if old:
                    o_out(old, 1)
                if ln:
                    fT_out(ln)
                if t:
                    exp_near(t, 1)
                    exp_far(t, 1)
                if new:
                    xnT_out(new)
                if t:
                    exp_near(t, 2)
                if ln or last:
                    affinities_and_ranks_out(i.plus(-3), ln, last)
                if t:
                    exp_far(t, 2)
                if nxt:
                    shift_out(nxt, 0)
                if nxt:
                    v_out(nxt)
                if t:
                    o_out(t, 0)
                if t:
                    exp_near(t, 3)
                if old:
                    onT_out(old)
                if t:
                    exp_far(t, 3)
                if new:
                    high(new)
                if ln:
                    exp_negative(ln)
                if new:
                    middle(new)

            iterations(act, step)

            act.wait_ge(s["ends_d"], 1)
            pad(act, range(1, E, 2))

            def normalise(t):
                q = t.slot(UT)
                act.wait_ge(xs_in[q], t.turns(UT, 16, 16))
                if t.follows(2):
                    act.wait_ge(s["xsT_r"], t.times(1, -1))
                a.activation(nh[:, t.slot(2)], xs[:, q, 0:D], ACT.Identity, scale=xs[:, q, RSTD:RSTD + 1],
                             bias=xs[:, q, SHFT:SHFT + 1]).then_inc(s["nh_d"], 1)

            def apply(t):
                p = t.slot(2)
                act.wait_ge(s["nb_z"], t.times(1, 1))
                if t.follows(2):
                    act.wait_ge(s["zo_d"], t.times(1, -1))
                a.activation(zn[:, p], zf[:, p], ACT.Identity, scale=rsz[:, p:p + 1], bias=nbz[:, p:p + 1])\
                    .then_inc(s["zn_d"], 1)

            def enter(t):
                p = t.slot(2)
                act.wait_ge(s["w1_d"], t.times(1, 1))
                act.wait_ge(s["xsT_r"], t.times(1, 1))
                if t.follows(2):
                    act.wait_ge(s["h_r"], t.times(2, -2))
                a.activation(nT[:, p], (M, ST1[:, 0])[p][:, 0:P], ACT.Identity, scale=w1s[:, p, F:F + 1],
                             bias=w1s[:, p, F + 1:F + 2]).then_inc(s["nT_d"], 1)

            def relu(t):
                p = t.slot(2)
                act.wait_ge(s["h_r"], t.times(2, 1))
                if t.follows(2):
                    act.wait_ge(s["z_r"], t.times(1, -1))
                for c in range(NA):
                    last = a.activation(hs[:, p, c], hidden(p, c), ACT.Relu, bias=w1s[:, p, F + 2 + c:F + 3 + c])
                last.then_inc(s["ha_d"], 1)

            def tile_step(t):
                if n := tile(t, 3):
                    normalise(n)
                if n := tile(t, 2):
                    enter(n)
                if n := tile(t, 1):
                    relu(n)
                if n := tile(t, -2):
                    apply(n)

            tiles(act, tile_step)

        @block.tensor
        def _(pe):
            mm = nc.tensor.matmul
            m_free = [[]]

            def take_m():
                for name, value in m_free[0]:
                    pe.wait_ge(s[name], value)

            def transpose_x(b):
                take_m()
                pe.wait_ge(s["xn_r"], b.times(1, 1))
                for t in (0, 1):
                    last = nc.tensor.transpose(M[:, t * P:(t + 1) * P], xn[:, b.slot(RING), t], ident[:, :])
                last.then_inc(s["xnT_r"], 1)
                m_free[0] = [("xnT_d", b.times(1, 1))]

            def project_qk(b):
                take_m()
                pe.wait_ge(s["xnT_d"], b.times(1, 1))
                for w in (0, 1):
                    last = mm(M[:, w * SEQ:(w + 1) * SEQ], wat[:, w], xnT[:, b.slot(RING)], start=True, stop=True)
                last.then_inc(s["qk_r"], 1)
                m_free[0] = [("hi_d", b.times(1, 1)), ("r1_d", b.times(1, 1))]

            def project_v(b):
                take_m()
                for t in (0, 1):
                    last = mm(M[:, t * P:(t + 1) * P], xnT[:, b.slot(RING), t * P:(t + 1) * P], wat[:, 2],
                              start=True, stop=True)
                last.then_inc(s["v_r"], 1)
                m_free[0] = [("v_d", b.times(1, 1))]

            def transpose_shift(b, half):
                take_m()
                pe.wait_ge(s["nm_d"], b.times(2, half + 1))
                nc.tensor.transpose(M[:, 0:P // 2].bitcast(BF16)[0:32, 0:P],
                                    nmp[:, b.slot(RING), half].rearrange("p c r -> p (c r)"), identb[:, :]).then_inc(s["shT_r"], 1)
                m_free[0] = [("sh_d", b.times(2, half + 1))]

            def scores_by_query(b, gr, u):
                p = b.slot(RING)
                n = 3 * gr + u
                if n == 0:
                    pe.wait_ge(aug_in[p], b.turns(RING, 96, 96))
                if b.k > 0 or n >= 2:
                    pe.wait_ge(s["red"], b.times(12, n - 1))
                bank = S[:, n % 2]
                q, k = qaug[0:SHIFT, p], kaug[0:SHIFT, p]
                if u == 0:
                    mm(bank, identb[:, :], causal[:, :, :], start=True, stop=False)
                    for j in range(4):
                        h = 4 * gr + j
                        last = mm(bank[:, j * P:(j + 1) * P], q[:, h, 0:P], k[:, h, 0:P], start=False, stop=(j == 3))
                else:
                    mm(bank.rearrange("p (j c n) -> p j c n", j=2, c=2)[:, :, 1], identb[:, :], causal[:, 0:2],
                       start=True, stop=False)
                    for j in range(2):
                        h = 4 * gr + 2 * (u - 1) + j
                        for kb in (0, 1):
                            last = mm(bank[:, j * SEQ + kb * P:j * SEQ + (kb + 1) * P], q[:, h, P:SEQ],
                                      k[:, h, kb * P:(kb + 1) * P], start=False, stop=(j == 1 and kb == 1))
                last.then_inc(s["s_r"], 1)

            def scores_near(i, gr):
                p = i.slot(RING)
                if gr % 2 == 0:
                    pe.wait_ge(sh_in[gr // 2], i.times(16, 16))
                if i.k > 0 or gr > 0:
                    pe.wait_ge(s["exp0"], i.times(NG, gr))
                for j in range(4):
                    h = 4 * gr + j
                    last = mm(ST0[:, j], kaug[:, p, h, 0:P], qaug[:, p, h], start=True, stop=True)
                last.then_inc(s["st0_r"], 1)

            def scores_far(i, gr):
                p = i.slot(RING)
                if i.k > 0 or gr > 0:
                    pe.wait_ge(s["exp1"], i.times(NG, gr))
                for j in range(4):
                    h = 4 * gr + j
                    last = mm(ST1[:, j], kaug[:, p, h, P:SEQ], qaug[:, p, h, P:SEQ], start=True, stop=True)
                last.then_inc(s["st1_r"], 1)

            def weigh_values(i, gr):
                p = i.slot(RING)
                if gr == 0:
                    pe.wait_ge(s["v_d"], i.times(1, 1))
                if i.k > 0 and gr % 2 == 0:
                    pe.wait_ge(s["o_ev"], i.times(2, gr // 2 - 1))
                pe.wait_ge(s["sel0"], i.times(NG, gr + 1))
                for j in range(4):
                    mm(O[32 * j:32 * j + 32, gr // 2, gr % 2, :], vaug[:, p, 0, 4 * gr + j], p0[:, gr % 2, j],
                       start=True, stop=False)
                pe.wait_ge(s["sel1"], i.times(NG, gr + 1))
                for j in range(4):
                    last = mm(O[32 * j:32 * j + 32, gr // 2, gr % 2, P:SEQ], vaug[:, p, 1, 4 * gr + j], p1[:, gr % 2, j],
                              start=False, stop=True)
                last.then_inc(s["pv"], 1)

            def transpose_o(i, qb):
                take_m()
                pe.wait_ge(s["o_ev"], i.times(2, 2))
                for gr in range(NG):
                    last = nc.tensor.transpose(M[:, gr * P:(gr + 1) * P], oT[:, gr, qb * P:(qb + 1) * P], ident[:, :])
                last.then_inc(s["otr_r"], 1)
                m_free[0] = [("on_d", i.times(2, qb + 1))]

            def transpose_on(i):
                take_m()
                pe.wait_ge(s["on_d"], i.times(2, 2))
                for qb in (0, 1):
                    last = nc.tensor.transpose(M[:, qb * P:(qb + 1) * P], on[:, qb].rearrange("p h v -> p (h v)"), ident[:, :])
                last.then_inc(s["onT_r"], 1)
                m_free[0] = [("onT_d", i.times(1, 1))]

            def project_o(i):
                take_m()
                for qb in (0, 1):
                    last = mm(M[:, qb * P:(qb + 1) * P], onT[:, qb * P:(qb + 1) * P], wat[:, 3], start=True, stop=True)
                last.then_inc(s["y_r"], 1)
                m_free[0] = [("y_d", i.times(1, 1))]

            def transpose_f(i):
                take_m()
                pe.wait_ge(s["f_d"], i.times(1, 1))
                for t in (0, 1):
                    last = nc.tensor.transpose(M[:, t * P:(t + 1) * P], pay[:, i.slot(RING), t, 0:D], ident[:, :])
                last.then_inc(s["fT_r"], 1)
                m_free[0] = [("fT_d", i.times(1, 1))]

            def affinities_and_ranks(n, ln, last):
                take_m()
                if ln:
                    pe.wait_ge(s["fT_d"], ln.times(1, 1))
                    if ln.k == 0:
                        pe.wait_ge(s["w_cent"], 16)
                    for t in (0, 1):
                        ins = mm(M[:, t * E:(t + 1) * E], fT[:, t], cent[:, :], start=True, stop=True)
                if last:
                    pe.wait_ge(s["run_d"], last.times(2, 2))
                    rank_m = M[:, 2 * E:4 * E].rearrange("p (t e) -> p t e", e=E)
                    mm(rank_m, before[:, :], last.pick(hot, 2, 2), start=True, stop=False)
                    ins = mm(rank_m, ones[:, :], last.pick(run, 2, 2), start=False, stop=True)
                ins.then_inc(s["ar_r"], 1)
                m_free[0] = [("ar_d", n.times(1, 1))]

            pe.wait_ge(s["consts"], 2)
            pe.wait_ge(s["w_attn"], 16)
            for n in (0, 1):
                transpose_x(Nth(n))
                project_qk(Nth(n))
                if n == 0:
                    project_v(Nth(n))
            transpose_x(Nth(2))
            pe.wait_ge(s["consts"], 6)
            for gr in range(NG):
                for u in range(3):
                    scores_by_query(Nth(0), gr, u)
                if gr == 1:
                    transpose_shift(Nth(0), 0)
                if gr == 2:
                    project_qk(Nth(2))

            def step(i):
                t, new, nxt, old, l2, ln, last = (at(i, n) for n in (0, 3, 1, -1, -2, -3, -4))
                if UB < i.k < B - 2:
                    m_free[0] = [("hi_d", i.times(1, 3)), ("r1_d", i.times(1, 3))]
                for gr in range(NG):
                    if t:
                        scores_near(t, gr)
                    if nxt:
                        scores_by_query(nxt, gr, 0)
                    if gr == 0 and l2:
                        project_o(l2)
                    if gr == 1 and old:
                        transpose_o(old, 0)
                    if gr == 2 and (ln or last):
                        affinities_and_ranks(i.plus(-3), ln, last)
                    if gr == 3 and old:
                        transpose_on(old)
                    if t:
                        scores_far(t, gr)
                    if nxt:
                        scores_by_query(nxt, gr, 1)
                    if gr == 0 and t:
                        transpose_shift(t, 1)
                    if gr == 0 and old:
                        weigh_values(old, 3)
                    if gr == 0 and ln:
                        transpose_f(ln)
                    if gr > 0 and t:
                        weigh_values(t, gr - 1)
                    if gr == 1 and old:
                        transpose_o(old, 1)
                    if gr == 2 and nxt:
                        transpose_shift(nxt, 0)
                    if gr == 3 and new:
                        project_qk(new)
                    if nxt:
                        scores_by_query(nxt, gr, 2)
                    if gr == 1 and new:
                        transpose_x(new)
                    if gr == 2 and nxt:
                        project_v(nxt)

            iterations(pe, step)

            take_m()
            mm(M[:, 0:E], ones[:, :], run[:, NT], start=True, stop=True).then_inc(s["total_r"], 1)
            pe.wait_ge(s["rt"], 1)

            def enter(t):
                p = t.slot(2)
                pe.wait_ge(s["nh_d"], t.times(1, 1))
                if t.follows(2):
                    pe.wait_ge(s["nT_d"], t.times(1, -1))
                nc.tensor.transpose((M, ST1[:, 0])[p][:, 0:P], nh[:, p], ident[:, :]).then_inc(s["xsT_r"], 1)

            def up(t):
                p = t.slot(2)
                pe.wait_ge(s["nT_d"], t.times(1, 1))
                for c in range(FC):
                    if t.follows(2) and c in (0, NA):
                        pe.wait_ge(s["hd_d" if c else "ha_d"], t.times(1, -1))
                    last = mm(hidden(p, c), w1s[:, p, c * P:(c + 1) * P], nT[:, p], start=True, stop=True)
                    if c in (NA - 1, FC - 1):
                        last.then_inc(s["h_r"], 1)

            def down_(t):
                p = t.slot(2)
                e = expert(pe, t)
                pe.wait_ge(s["ha_d"], t.times(1, 1))
                if t.follows(2):
                    pe.wait_ge(s["zb_d"], t.times(1, -1))
                for c in range(FC):
                    if c == NA:
                        pe.wait_ge(s["hd_d"], t.times(1, 1))
                    last = mm(O[:, p, 0, 0:D], hs[:, p, c], w2_tab[:, bass.ds(e * (FC * D) + c * D, D)],
                              start=(c == 0), stop=(c == FC - 1))
                last.then_inc(s["z_r"], 1)

            def tile_step(t):
                if n := tile(t, 2):
                    enter(n)
                if n := tile(t, 1):
                    up(n)
                if n := tile(t, 0):
                    down_(n)

            tiles(pe, tile_step)

        @block.vector
        def _(dve):
            v = nc.vector

            def x_stats(n, k=None):
                lo, hi = STATS[n]
                if k is not None:
                    lo, hi = lo + k, min(lo + k + 1, hi)
                for t in range(lo, hi):
                    ins = v.bn_stats(stx[:, t], x_all[:, t])
                    if t == STATS[n][1] - 1:
                        ins.then_inc(s["st_x"], 1)

            def x_variance(n):
                lo, hi = STATS[n]
                dve.wait_ge(s["st_x"], n + 1)
                for t in range(lo, hi):
                    last = v.bn_aggr(mvx[:, t], stx[:, t])
                last.then_inc(s["agg_x"], 1)
                dve.wait_ge(s["agg_x"], n + 1)
                v.tensor_scalar_add(vex[:, lo:hi], mvx[:, lo:hi, 1], EPS).then_inc(s["ve_x"], 1)

            v.memset(qaug[:, 0].bitcast(F32), 0.0).then_inc(s["qzero"], 1)
            dve.wait_ge(s["x_in"], 16)
            x_stats(0)
            x_variance(0)

            def normalise_x(b):
                p = b.slot(RING)
                if b.follows(RING):
                    dve.wait_ge(s["xnT_r"], b.times(1, 1 - RING))
                for t in (0, 1):
                    src = b.pick(x_all, 1, 2, t).rearrange("p o d -> p (o d)")
                    last = v.tensor_scalar(xn[:, p, t], src, b.pick(mvx, 1, 2, t)[:, :, 0], b.pick(rsx, 1, 2, t),
                                           ALU.subtract, ALU.mult)
                last.then_inc(s["xn_r"], 1)

            def residue(b):
                dve.wait_ge(s["hi_d"], b.times(1, 1))
                if b.follows(1):
                    dve.wait_ge(s["parts_d"], b.times(1))
                v.tensor_tensor(res1[:, :, :], M[:, :].rearrange("p (s t) -> p s t", s=2), part(b.slot(RING), 0),
                                ALU.subtract).then_inc(s["r1_d"], 1)

            def maxima(b, gr, u):
                p = b.slot(RING)
                n = 3 * gr + u
                dve.wait_ge(s["s_r"], b.times(12, n + 1))
                if u == 0:
                    dst, k = nmf[:, p, 4 * gr:4 * gr + 4, 0], 4
                else:
                    dst, k = nmf[:, p, 4 * gr + 2 * (u - 1):4 * gr + 2 * u, 1], 2
                v.tensor_reduce(dst, S[:, n % 2].rearrange("p (j n) -> p j n", j=k), op=ALU.max, axis=AX_X,
                                negate=True).then_inc(s["red"], 1)

            def maxima_and_stats(i, b, gr, u):
                maxima(b, gr, u)
                if i.k < 2:
                    x_stats(i.k + 3, 3 * gr + u)

            def shift_parts(b, half):
                p = b.slot(RING)
                src = nmf[:, p, 8 * half:8 * half + 8].rearrange("p h q -> p (h q)")
                dve.wait_ge(s["red"], b.times(12, 6 * half + 6))
                if b.follows(RING):
                    dve.wait_ge(s["shT_r"], b.times(2, half + 1 - 2 * RING))
                v.tensor_copy(nmp[:, p, half, 0], src).then_inc(s["nm_hi"], 1)
                dve.wait_ge(s["nm_hi"], b.times(2, half + 1))
                v.tensor_tensor(nmp[:, p, half, 1], src, nmp[:, p, half, 0], ALU.subtract).then_inc(s["nm_d"], 1)

            def divide(i, qb):
                mo = M[:, :].rearrange("p (h n) -> p h n", n=32)
                dve.wait_ge(s["otr_r"], i.times(2, qb + 1))
                v.reciprocal(rden[:, qb], mo[:, :, DH]).then_inc(s["rden_d"], 1)
                dve.wait_ge(s["rden_d"], i.times(2, qb + 1))
                if i.follows(1):
                    dve.wait_ge(s["onT_r"], i.times(1))
                v.tensor_tensor(on[:, qb], mo[:, :, 0:DH], rden[:, qb].unsqueeze(2).to_broadcast([P, NH, DH]),
                                ALU.mult).then_inc(s["on_d"], 1)

            def ln_src(b, n):
                if n == 0:
                    return lambda t: yb[:, b.slot(RING), t]
                if n == 1:
                    return lambda t: pay[:, b.slot(RING), t, D:2 * D]
                return lambda t: pay[:, b.slot(RING), t, 0:D]

            def ln_stats(b, n):
                wait_fixed(dve, s[("y_d", "x2_d", "f_d")[n]], b.times(1, 1))
                for t in (0, 1):
                    last = v.bn_stats(st_ln[:, n, t], ln_src(b, n)(t))
                last.then_inc(s["ln_st"], 1)

            def ln_aggregate(b, n):
                wait_fixed(dve, s["ln_st"], b.times(3, n + 1))
                for t in (0, 1):
                    dst = mv_ln[:, n, t] if n < 2 else pay[:, b.slot(RING), t, MEAN:MEAN + 2]
                    last = v.bn_aggr(dst, st_ln[:, n, t])
                last.then_inc(s["ln_ag"], 1)

            def ln_variance(b, n):
                dve.wait_ge(s["ln_ag"], b.times(3, n + 1))
                var = mv_ln[:, n, :, 1] if n < 2 else pay[:, b.slot(RING), :, VAR]
                v.tensor_scalar_add(ve_ln[:, n], var, EPS).then_inc(s["ln_ve"], 1)

            def ln_apply(b, n, dst, done):
                dve.wait_ge(s["ln_rs"], b.times(3, n + 1))
                for t in (0, 1):
                    last = v.tensor_scalar(dst(t), ln_src(b, n)(t), mv_ln[:, n, t, 0:1], rs_ln[:, n, t:t + 1],
                                           ALU.subtract, ALU.mult)
                last.then_inc(s[done], 1)

            def add_y(b):
                dve.wait_ge(s["yn_d"], b.times(1, 1))
                p = b.slot(RING)
                if b.follows(RING) or p == FIRST_SCAT:
                    dve.wait_ge(scat[p], b.turns(RING, 32, 16 * (p == FIRST_SCAT)))
                v.tensor_tensor(pay[:, p, :, D:2 * D], b.pick(x_all, 2, 2), yn[:, :, :], ALU.add).then_inc(s["x2_d"], 1)

            def choose(b, n):
                if n == 0:
                    dve.wait_ge(s["ar_d"], b.times(1, 1))
                    v.tensor_reduce(b.pick(amax, 2, 2), b.pick(aff, 2, 2), op=ALU.max, axis=AX_X).then_inc(s["chosen"], 1)
                    return
                dve.wait_ge(s["chosen"], b.times(4, n))
                if n == 1:
                    for t in (0, 1):
                        last = v.scalar_tensor_tensor(
                            out=b.pick(hotk, 1, 2, t).rearrange("p o e -> p (o e)"),
                            in0=b.pick(aff, 1, 2, t).rearrange("p o e -> p (o e)"),
                            scalar=b.pick(amax, 1, 2, t), in1=down[:, :], op0=ALU.is_equal, op1=ALU.mult)
                if n == 2:
                    last = v.tensor_reduce(b.pick(key, 2, 2), b.pick(hotk, 2, 2), op=ALU.max, axis=AX_X)
                if n == 3:
                    last = v.tensor_tensor(b.pick(hot, 2, 2), down[:, :].unsqueeze(1).to_broadcast([P, 2, E]),
                                           b.pick(key, 2, 2).unsqueeze(2).to_broadcast([P, 2, E]), ALU.is_equal)
                last.then_inc(s["chosen"], 1)

            def count(b, t):
                if t == 0:
                    dve.wait_ge(s["chosen"], b.times(4, 4))
                if t or b.follows(1):
                    dve.wait_ge(s["run_d"], b.times(2, t))
                v.tensor_tensor(b.pick(run, 1, 2, t + 1), b.pick(run, 1, 2, t), b.pick(hot, 1, 2, t), ALU.add)\
                    .then_inc(s["run_d"], 1)

            def alphas(b, n):
                if n == 0:
                    dve.wait_ge(s["ex_d"], b.times(1, 1))
                    v.tensor_scalar_add(b.pick(eneg, 2, 2), b.pick(eneg, 2, 2), 1.0).then_inc(s["al_p"], 1)
                else:
                    wait_fixed(dve, s["al_p"], b.times(1, 1))
                    v.reciprocal(pay[:, b.slot(RING), :, ALPHA], b.pick(eneg, 2, 2)).then_inc(s["al_d"], 1)

            def ln_shift(b):
                row = pay[:, b.slot(RING)]
                dve.wait_ge(s["ln_rs"], b.times(3, 3))
                v.scalar_tensor_tensor(out=row[:, :, SHFT], in0=row[:, :, MEAN], scalar=-1.0, in1=row[:, :, RSTD],
                                       op0=ALU.mult, op1=ALU.mult).then_inc(s["ln_sh"], 1)

            def place(b, n):
                if n == 0:
                    dve.wait_ge(s["ar_d"], b.times(1, 2))
                    v.tensor_tensor(b.pick(posw, 2, 2), b.pick(rank, 2, 2), b.pick(hot, 2, 2),
                                    ALU.mult).then_inc(s["pw_d"], 1)
                if n == 1:
                    dve.wait_ge(s["pw_d"], b.times(1, 1))
                    v.tensor_reduce(b.pick(posf, 2, 2), b.pick(posw, 2, 2), op=ALU.add, axis=AX_X).then_inc(s["pf_d"], 1)
                if n == 2:
                    wait_fixed(dve, s["pf_d"], b.times(1, 1))
                    v.tensor_copy(pos[:, b.slot(RING)], b.pick(posf, 2, 2)).then_inc(s["pos_d"], 1)

            dve.wait_ge(s["rs_x"], 1)
            normalise_x(Nth(0))
            dve.wait_ge(s["x_next"], 16)
            x_stats(1)
            x_variance(1)
            v.memset(vaug[:, 0], 0.0).then_inc(s["vmem"], 1)
            dve.wait_ge(s["vmem"], 1)
            v.memset(vaug[:, 0, :, :, DH:DH + 1], 1.0).then_inc(s["vones"], 1)
            dve.wait_ge(s["rs_x"], 2)
            normalise_x(Nth(1))
            residue(Nth(0))
            v.memset(qaug[:, 1].bitcast(F32), 0.0).then_inc(s["qzero"], 1)
            v.memset(qaug[:, 2].bitcast(F32), 0.0).then_inc(s["qzero"], 1)
            residue(Nth(1))
            normalise_x(Nth(2))
            dve.wait_ge(s["x_rest"], 16)
            x_stats(2)
            x_variance(2)
            v.memset(vaug[:, 1], 0.0)
            v.memset(vaug[:, 2], 0.0).then_inc(s["vmem"], 1)
            dve.wait_ge(s["vmem"], 2)
            v.memset(vaug[:, 1, :, :, DH:DH + 1], 1.0).then_inc(s["vones"], 1)
            v.memset(vaug[:, 2, :, :, DH:DH + 1], 1.0).then_inc(s["vones"], 1)
            for gr in range(NG):
                for u in range(3):
                    maxima(Nth(0), gr, u)
                if gr % 2:
                    shift_parts(Nth(0), gr // 2)
                if gr == 2:
                    residue(Nth(2))
            dve.wait_ge(s["rs_x"], 3)

            def step(i):
                new, nxt, old = at(i, 3), at(i, 1), at(i, -1)
                l2, l3, l4 = at(i, -2), at(i, -3), at(i, -4)
                if i.k in (3, 6):
                    dve.wait_ge(s["rs_x"], 4 if i.k == 3 else 5)
                if nxt:
                    maxima_and_stats(i, nxt, 0, 0)
                if nxt:
                    maxima_and_stats(i, nxt, 0, 1)
                if l4:
                    alphas(l4, 0)
                if l2:
                    ln_stats(l2, 0)
                if nxt:
                    maxima_and_stats(i, nxt, 0, 2)
                if l4:
                    alphas(l4, 1)
                if new:
                    normalise_x(new)
                if l2:
                    ln_aggregate(l2, 0)
                if nxt:
                    maxima_and_stats(i, nxt, 1, 0)
                if old:
                    divide(old, 0)
                if nxt:
                    maxima_and_stats(i, nxt, 1, 1)
                if l2:
                    ln_variance(l2, 0)
                if old:
                    divide(old, 1)
                if nxt:
                    maxima_and_stats(i, nxt, 1, 2)
                if l2:
                    if l2.follows(1):
                        dve.wait_ge(s["x2_d"], l2.times(1))
                    ln_apply(l2, 0, lambda t: yn[:, t], "yn_d")
                if nxt:
                    maxima_and_stats(i, nxt, 2, 0)
                    shift_parts(nxt, 0)
                if l2:
                    add_y(l2)
                if nxt:
                    maxima_and_stats(i, nxt, 2, 1)
                if l2:
                    ln_stats(l2, 1)
                if l4:
                    place(l4, 0)
                if l3:
                    choose(l3, 0)
                    ln_shift(l3)
                if l2:
                    ln_aggregate(l2, 1)
                if nxt:
                    maxima_and_stats(i, nxt, 2, 2)
                if l4:
                    place(l4, 1)
                if l3:
                    choose(l3, 1)
                if l2:
                    ln_variance(l2, 1)
                if nxt:
                    maxima_and_stats(i, nxt, 3, 0)
                if l4:
                    place(l4, 2)
                if l3:
                    choose(l3, 2)
                if nxt:
                    maxima_and_stats(i, nxt, 3, 1)
                if l3:
                    choose(l3, 3)
                if l2:
                    ln_apply(l2, 1, lambda t: pay[:, l2.slot(RING), t, 0:D], "f_d")
                if nxt:
                    maxima_and_stats(i, nxt, 3, 2)
                if new:
                    residue(new)
                if nxt:
                    shift_parts(nxt, 1)
                if l3:
                    count(l3, 0)
                if l2:
                    ln_stats(l2, 2)
                if l3:
                    count(l3, 1)
                if l2:
                    ln_aggregate(l2, 2)
                    ln_variance(l2, 2)
                if i.k < 2:
                    x_variance(i.k + 3)

            iterations(dve, step)

            chain = [0]

            def link(ins):
                chain[0] += 1
                ins.then_inc(s["tl"], 1)
                dve.wait_ge(s["tl"], chain[0])

            dve.wait_ge(s["total_r"], 1)
            v.tensor_copy(ends[:, :], M[:, 0:E]).then_inc(s["ends_d"], 1)
            link(v.tensor_tensor(cnt[:, :], M[:, 0:E], starts[:, :], ALU.subtract))
            link(v.tensor_tensor(above[:, :, :], cnt[:, :].unsqueeze(2).to_broadcast([P, E, NT]),
                                 steps[:, :].unsqueeze(1).to_broadcast([P, E, NT]), ALU.is_gt))
            link(v.tensor_reduce(ntile[:, 0], above[:, :, :], op=ALU.add, axis=AX_X))
            cur, n = 0, 1
            while n < E:
                v.tensor_copy(ntile[:, cur + 1, 0:n], ntile[:, cur, 0:n])
                link(v.tensor_tensor(ntile[:, cur + 1, n:E], ntile[:, cur, n:E], ntile[:, cur, 0:E - n], ALU.add))
                cur, n = cur + 1, 2 * n
            v.tensor_scalar(skip[:, :], ntile[:, 0], -float(P), float(CAP), ALU.mult, ALU.add)
            link(v.tensor_tensor(over[:, 0], slots[:, :].unsqueeze(2).to_broadcast([P, ST, E]),
                                 ntile[:, cur].unsqueeze(1).to_broadcast([P, ST, E]), ALU.is_ge))
            v.tensor_tensor(over[:, 1], over[:, 0], skip[:, :].unsqueeze(1).to_broadcast([P, ST, E]), ALU.mult)
            link(v.tensor_reduce(esel[:, :], over[:, 0], op=ALU.add, axis=AX_X))
            v.tensor_scalar(eidx[:, :], esel[:, :], float(E - 1), None, ALU.min)
            link(v.tensor_reduce(rowf[:, 0], over[:, 1], op=ALU.add, axis=AX_X))
            link(v.scalar_tensor_tensor(out=rowf[:, 1], in0=slots[:, :], scalar=float(P), in1=rowf[:, 0],
                                        op0=ALU.mult, op1=ALU.add))
            v.tensor_scalar(rows_at[:, :], rowf[:, 1], float(E * CAP), None, ALU.min).then_inc(s["rt"], 1)
            dve.wait_ge(s["rt"], 1)
            dve.wait_ge(s["w_ffn"], 16 * (2 * E + 3))

            kept = {}

            def weights(t):
                p = t.slot(2)
                e = kept[id(t.trip), t.k]
                if t.follows(2):
                    dve.wait_ge(s["h_r"], t.times(2, -2))
                    dve.wait_ge(s["ha_d"], t.times(1, -1))
                    dve.wait_ge(s["hd_d"], t.times(1, -1))
                v.tensor_copy(w1s[:, p], w1_tab[:, bass.ds(e, 1), :].rearrange("p o n -> p (o n)")).then_inc(s["w1_d"], 1)

            def relu(t):
                p = t.slot(2)
                dve.wait_ge(s["w1_d"], t.times(1, 1))
                dve.wait_ge(s["h_r"], t.times(2, 2))
                if t.follows(2):
                    dve.wait_ge(s["z_r"], t.times(1, -1))
                for c in range(NA, FC):
                    last = v.tensor_scalar(hs[:, p, c], hidden(p, c), w1s[:, p, F + 2 + c:F + 3 + c], 0.0, ALU.add, ALU.max)
                last.then_inc(s["hd_d"], 1)

            def add_bias(t):
                p = t.slot(2)
                e = kept.pop((id(t.trip), t.k), None)
                if e is None:
                    e = expert(dve, t)
                dve.wait_ge(s["z_r"], t.times(1, 1))
                v.tensor_tensor(zb[:, p], O[:, p, 0, 0:D], b2_tab[:, bass.ds(e * D, D)], ALU.add).then_inc(s["zb_d"], 1)

            def residual(t):
                p, q = t.slot(2), t.slot(UT)
                dve.wait_ge(s["zb_d"], t.times(1, 1))
                if t.follows(2):
                    dve.wait_ge(s["zn_d"], t.times(1, -1))
                v.scalar_tensor_tensor(out=zf[:, p], in0=zb[:, p], scalar=xs[:, q, ALPHA:ALPHA + 1], in1=xs[:, q, 0:D],
                                       op0=ALU.mult, op1=ALU.add).then_inc(s["zf_d"], 1)

            def statistics(t):
                wait_fixed(dve, s["zf_d"], t.times(1, 1))
                v.bn_stats(stz[:, t.slot(2)], zf[:, t.slot(2)]).then_inc(s["st_z"], 1)

            def aggregate(t):
                wait_fixed(dve, s["st_z"], t.times(1, 1))
                v.bn_aggr(mvz[:, t.slot(2)], stz[:, t.slot(2)]).then_inc(s["agg_z"], 1)

            def variance(t):
                p = t.slot(2)
                dve.wait_ge(s["agg_z"], t.times(1, 1))
                v.tensor_scalar_add(vez[:, p:p + 1], mvz[:, p, 1:2], EPS).then_inc(s["ve_z"], 1)

            def z_bias(t):
                p = t.slot(2)
                dve.wait_ge(s["rs_z"], t.times(1, 1))
                v.scalar_tensor_tensor(out=nbz[:, p:p + 1], in0=mvz[:, p, 0:1], scalar=-1.0, in1=rsz[:, p:p + 1],
                                       op0=ALU.mult, op1=ALU.mult).then_inc(s["nb_z"], 1)

            def add_x(t):
                p, q = t.slot(2), t.slot(UT)
                dve.wait_ge(s["zn_d"], t.times(1, 1))
                if t.follows(2):
                    dve.wait_ge(out_s[p], t.turns(2, 16))
                v.tensor_copy(ids[:, p:p + 1], xs[:, q, TOK:TOK + 1].bitcast(I32))
                v.tensor_tensor(zo[:, p], zn[:, p], xs[:, q, D:2 * D], ALU.add).then_inc(s["zo_d"], 1)

            def tile_step(t):
                if n := tile(t, -1):
                    residual(n)
                if n := tile(t, 1):
                    relu(n)
                if n := tile(t, 3):
                    kept[id(n.trip), n.k] = expert(dve, n)
                if n := tile(t, -1):
                    statistics(n)
                if n := tile(t, -2):
                    z_bias(n)
                if n := tile(t, 0):
                    add_bias(n)
                if n := tile(t, -1):
                    aggregate(n)
                if n := tile(t, -3):
                    add_x(n)
                if n := tile(t, -1):
                    variance(n)
                if n := tile(t, 3):
                    weights(n)

            tiles(dve, tile_step)


def kernel(L0_attn_x, L0_attn_WQ, L0_attn_WK, L0_attn_WV, L0_attn_WO, L0_ffn_centroids, L0_ffn_ln_g, L0_ffn_ln_b,
           L0_ffn_w1, L0_ffn_b1, L0_ffn_w2, L0_ffn_b2):
    import concourse.bacc as bacc
    from concourse.bass_utils import run_bass_kernel_spmd

    nh, dh, d = L0_attn_WQ.shape
    e, f, _ = L0_ffn_w1.shape
    attn_w = np.stack([np.asarray(w).transpose(2, 1, 0).reshape(d, nh * dh) for w in (L0_attn_WQ, L0_attn_WK)]
                      + [np.asarray(L0_attn_WV).reshape(nh * dh, d).T]
                      + [np.asarray(L0_attn_WO).transpose(0, 2, 1).reshape(nh * dh, d)])
    w1t = np.asarray(L0_ffn_w1).transpose(0, 2, 1)
    w2t = np.asarray(L0_ffn_w2).reshape(e, d, f // 128, 128).transpose(3, 0, 2, 1).reshape(128, -1)
    ln_cols = np.stack([np.asarray(L0_ffn_ln_g), np.asarray(L0_ffn_ln_b)], axis=-1).transpose(1, 0, 2)
    b1_cols = np.asarray(L0_ffn_b1).reshape(e, f // 128, 128).transpose(2, 0, 1)
    arrays = {"x": L0_attn_x, "attn_w": attn_w, "w1t": w1t, "w2t": w2t, "ln_cols": ln_cols, "b1_cols": b1_cols,
              "b2": L0_ffn_b2, "cent_t": np.asarray(L0_ffn_centroids).T}
    nc = bacc.Bacc("TRN2", target_bir_lowering=False, num_devices=1)
    ins, args = {}, {}
    for name, value in arrays.items():
        value = np.ascontiguousarray(value)
        ins[f"in_{name}"] = value
        args[name] = nc.dram_tensor(f"in_{name}", value.shape, mybir.dt.from_np(value.dtype), kind="ExternalInput").ap()
    out = nc.dram_tensor("out_x", tuple(L0_attn_x.shape), F32, kind="ExternalOutput").ap()
    sandwich_kernel(nc, out=out, **args)
    return run_bass_kernel_spmd(nc, [ins], core_ids=[0]).results[0]["out_x"]
```
